# Optimizing a Trainium2 kernel written in Bass

```python
import numpy as np
import jax
import jax.numpy as jnp

def _softmax(x, axis=-1):
    return jax.nn.softmax(x, axis=axis)

def _gelu(x):
    return jax.nn.gelu(x, approximate=True)

def _silu(x):
    return jax.nn.silu(x)

def _sigmoid(x):
    return jax.nn.sigmoid(x)

def _layernorm(x, axis=-1, eps=1e-05):
    m = jnp.mean(x, axis=axis, keepdims=True)
    v = jnp.var(x, axis=axis, keepdims=True)
    return (x - m) / jnp.sqrt(v + eps)

def _scatter_add(tgt, idx, src, axis=0):
    return tgt.at[idx].add(src)

def _segment_sum(src, seg, n):
    return jax.ops.segment_sum(src, seg, n)
kernel_name = 'mk_xattn_ffn_d1_seqx_r8_8edfad'

def setup_inputs(seed: int=0):
    np.random.seed(seed)
    _w = jnp.asarray

    def _rec_inputs():
        import jax
        import jax.numpy as jnp
        _rk = jax.random.key(seed)
        x = 7.22e-05 + 1 * jax.random.normal(jax.random.fold_in(_rk, 1), (32, 64, 256), jnp.float32)
        _lenS = 64 - jax.random.randint(jax.random.fold_in(_rk, 7), (32,), 0, max(1, 64 // 4) + 1, jnp.int32)
        _lenS2 = 64 - jax.random.randint(jax.random.fold_in(_rk, 8), (32,), 0, max(1, 64 // 4) + 1, jnp.int32)
        _ctx_2048P = jax.random.normal(jax.random.fold_in(_rk, 11), (32, 16, 256), jnp.float32)
        _ctx_2048c = jax.random.dirichlet(jax.random.fold_in(_rk, 511), 0.3 * jnp.ones((16,), jnp.float32), (32, 64))
        _ctx_2048t = jnp.einsum('bsk,bkd->bsd', _ctx_2048c, _ctx_2048P)
        _ctx_2048t = _ctx_2048t * jax.lax.rsqrt(jnp.mean(jnp.square(_ctx_2048t)) + 1e-12) * 0.953939
        ctx_2048 = 4.13588e-05 + 0.999923 * (_ctx_2048t + 0.3 * jax.random.normal(jax.random.fold_in(_rk, 611), (32, 64, 256), jnp.float32))
        return (x, ctx_2048)
    x, ctx_2048 = _rec_inputs()

    def _L0_xattn_setup():
        import jax, jax.numpy as jnp
        import numpy as np
        BS, S, DK = (8, 64, 256)
        key = jax.random.key(seed)
        kq, kk, kv = jax.random.split(key, 3)
        q = jax.random.normal(kq, (BS, S, DK), dtype=jnp.float32)
        k = jax.random.normal(kk, (BS, S, DK), dtype=jnp.float32)
        v = jax.random.normal(kv, (BS, S, DK), dtype=jnp.float32)
        return {'q': q, 'k': k, 'v': v}
    _L0_xattn_all = _L0_xattn_setup()
    _L0_xattn_in = {k: v for k, v in _L0_xattn_all.items() if k in ()}
    del _L0_xattn_all

    def _L0_ffn_setup():
        import jax, jax.numpy as jnp
        import numpy as np
        B, S, D = (2, 256, 256)
        E, I, TOPK = (64, 96, 8)
        M = B * S
        CAP = 2 * (M * TOPK) // E

        def _moe(x, router_weight, gate_proj, up_proj, down_proj):
            b, s, d = x.shape
            xf = x.reshape(-1, d)
            m = xf.shape[0]
            logits = xf @ router_weight
            probs = jax.nn.softmax(logits.astype(jnp.float32), axis=-1)
            topw, topi = jax.lax.top_k(probs, TOPK)
            topw = topw / topw.sum(axis=-1, keepdims=True)
            flat_e = topi.reshape(-1)
            flat_w = topw.reshape(-1).astype(x.dtype)
            order = jnp.argsort(flat_e)
            se = flat_e[order]
            tok = order // TOPK
            counts = jax.ops.segment_sum(jnp.ones_like(flat_e), flat_e, num_segments=E)
            starts = jnp.cumsum(counts) - counts
            pos = jnp.arange(m * TOPK) - starts[se]
            valid = pos < CAP
            posc = jnp.minimum(pos, CAP - 1)
            xe = jnp.zeros((E, CAP, d), x.dtype).at[se, pos].set(xf[tok], mode='drop')
            h = jax.nn.silu(jnp.einsum('ecd,edi->eci', xe, gate_proj)) * jnp.einsum('ecd,edi->eci', xe, up_proj)
            ye = jnp.einsum('eci,eid->ecd', h, down_proj)
            contrib = jnp.where(valid[:, None], ye[se, posc], 0.0) * flat_w[order][:, None]
            out = jnp.zeros((m, d), x.dtype).at[tok].add(contrib)
            return out.reshape(b, s, d)
        key = jax.random.key(seed)
        k0, k1, k2, k3, k4 = jax.random.split(key, 5)
        return {'x': jax.random.normal(k0, (B, S, D), jnp.float32), 'router_weight': jax.random.normal(k1, (D, E), jnp.float32) * 0.02, 'gate_proj': jax.random.normal(k2, (E, D, I), jnp.float32) * 0.02, 'up_proj': jax.random.normal(k3, (E, D, I), jnp.float32) * 0.02, 'down_proj': jax.random.normal(k4, (E, I, D), jnp.float32) * 0.02}
    _L0_ffn_all = _L0_ffn_setup()
    _L0_ffn_in = {k: v for k, v in _L0_ffn_all.items() if k in ('router_weight', 'gate_proj', 'up_proj', 'down_proj')}
    del _L0_ffn_all
    return {'x': x, 'ctx_2048': ctx_2048, 'L0_ffn_router_weight': _L0_ffn_in['router_weight'], 'L0_ffn_gate_proj': _L0_ffn_in['gate_proj'], 'L0_ffn_up_proj': _L0_ffn_in['up_proj'], 'L0_ffn_down_proj': _L0_ffn_in['down_proj']}

def reference(x, ctx_2048, L0_ffn_router_weight, L0_ffn_gate_proj, L0_ffn_up_proj, L0_ffn_down_proj):
    import jax
    import jax.numpy as jnp

    def _L0_xattn_ref(q, k, v):
        import jax, jax.numpy as jnp
        import numpy as np
        BS, S, DK = (8, 64, 256)
        dk = q.shape[-1]
        scale = 1.0 / jnp.sqrt(jnp.asarray(dk, dtype=q.dtype))
        scaled = jnp.einsum('bsd,bse->bde', q, k) * scale
        attn = jax.nn.softmax(scaled, axis=1)
        out = jnp.einsum('bde,bse->bsd', attn, v)
        return out

    def _L0_ffn_ref(x, router_weight, gate_proj, up_proj, down_proj):
        import jax, jax.numpy as jnp
        import numpy as np
        B, S, D = (2, 256, 256)
        E, I, TOPK = (64, 96, 8)
        M = B * S
        CAP = 2 * (M * TOPK) // E

        def _moe(x, router_weight, gate_proj, up_proj, down_proj):
            b, s, d = x.shape
            xf = x.reshape(-1, d)
            m = xf.shape[0]
            logits = xf @ router_weight
            probs = jax.nn.softmax(logits.astype(jnp.float32), axis=-1)
            topw, topi = jax.lax.top_k(probs, TOPK)
            topw = topw / topw.sum(axis=-1, keepdims=True)
            flat_e = topi.reshape(-1)
            flat_w = topw.reshape(-1).astype(x.dtype)
            order = jnp.argsort(flat_e)
            se = flat_e[order]
            tok = order // TOPK
            counts = jax.ops.segment_sum(jnp.ones_like(flat_e), flat_e, num_segments=E)
            starts = jnp.cumsum(counts) - counts
            pos = jnp.arange(m * TOPK) - starts[se]
            valid = pos < CAP
            posc = jnp.minimum(pos, CAP - 1)
            xe = jnp.zeros((E, CAP, d), x.dtype).at[se, pos].set(xf[tok], mode='drop')
            h = jax.nn.silu(jnp.einsum('ecd,edi->eci', xe, gate_proj)) * jnp.einsum('ecd,edi->eci', xe, up_proj)
            ye = jnp.einsum('eci,eid->ecd', h, down_proj)
            contrib = jnp.where(valid[:, None], ye[se, posc], 0.0) * flat_w[order][:, None]
            out = jnp.zeros((m, d), x.dtype).at[tok].add(contrib)
            return out.reshape(b, s, d)
        return _moe(x, router_weight, gate_proj, up_proj, down_proj)
    x = x + _L0_xattn_ref(_layernorm(x, axis=-1), ctx_2048, ctx_2048)
    x = x + _L0_ffn_ref(_layernorm(x, axis=-1), L0_ffn_router_weight, L0_ffn_gate_proj, L0_ffn_up_proj, L0_ffn_down_proj)
    return x

_drawn_inputs = setup_inputs


def setup_inputs(seed=0):
    import zlib

    import numpy as np

    out = dict(_drawn_inputs(seed))
    spreads = {}
    factors = {'L0_ffn_router_weight': 8.0,
     'L0_ffn_gate_proj': 8.0,
     'L0_ffn_up_proj': 8.0,
     'L0_ffn_down_proj': 8.0}
    for name, (base, spread) in spreads.items():
        noise = np.random.default_rng([zlib.crc32(name.encode()), seed]).standard_normal(out[name].shape)
        drawn = base * np.exp(spread * noise) if base else spread * noise
        out[name] = jnp.asarray(drawn.astype(out[name].dtype))
    for name, factor in factors.items():
        out[name] = (out[name] * factor).astype(out[name].dtype)
    return out
```

```python
from contextlib import ExitStack

import numpy as np

import concourse.bass as bass
from concourse import mybir

P = 128
BATCH, SEQ, D = 32, 64, 256
TOKENS = BATCH * SEQ
TILES = TOKENS // P
HALVES = P // SEQ
DC = D // P
EXPERTS, INNER, TOPK = 64, 96, 8
CAP = 2 * (512 * TOPK) // EXPERTS
ROW = D + EXPERTS
UNROLL = 4
RING = 4
SUMS = 2
GROUP = 8
GROUPS = EXPERTS // GROUP
EPS = 1e-5

F32 = mybir.dt.float32
F16 = mybir.dt.float16
I32 = mybir.dt.int32
U32 = mybir.dt.uint32
ALU = mybir.AluOpType
ACT = mybir.ActivationFunctionType
AX = mybir.AxisListType


def build(nc, tok, wgu, wd, wr, out):
    table = nc.dram_tensor("table", [TOKENS + P, ROW], F32, kind="Internal").ap()
    sums = [nc.dram_tensor(f"sum{n}", [TOKENS + P, D], F32, kind="Internal").ap() for n in range(SUMS)]
    out_rows = out.rearrange("b s d -> (b s) d")

    with ExitStack() as ctx:
        def sb(name, shape, dt=F32):
            return ctx.enter_context(nc.sbuf_tensor(name, shape, dt))

        def sem(name):
            return ctx.enter_context(nc.semaphore(name))

        wgu_sb = sb("wgu_sb", [P, EXPERTS, DC * 2 * INNER])
        wd_sb = sb("wd_sb", [INNER, EXPERTS, D])
        wr_sb = sb("wr_sb", [P, DC, EXPERTS])
        tok_sb = sb("tok_sb", [P, RING, 3 * D])
        xn = sb("xn", [P, 2, D])
        probs = sb("probs", [P, 2, HALVES * DC * D])
        vT = sb("vT", [P, 2, HALVES * DC * SEQ])
        x1 = sb("x1", [P, 2, D])
        row = sb("row", [P, RING, ROW])
        xnT = sb("xnT", [P, 2, D])
        slot_hot = sb("slot_hot", [P, 2, TOPK, CAP], F16)
        expert_hot = sb("expert_hot", [P, 2, TOPK, EXPERTS], F16)
        ident = sb("ident", [P, P])
        before = sb("before", [P, P], F16)
        ones = sb("ones", [P, P], F16)
        count = sb("count", [P, P], F16)
        count_i = sb("count_i", [P, P], I32)
        expert_base = sb("expert_base", [P, EXPERTS])
        token_no = sb("token_no", [P, TILES], I32)
        token_now = sb("token_now", [P, 2], I32)
        spare_i = sb("spare_i", [P, 1], I32)
        spare = sb("spare", [P, 1])
        eps = sb("eps", [P, 1])
        neg_half = sb("neg_half", [P, 1])
        stats1 = sb("stats1", [P, 2, 6])
        stats2 = sb("stats2", [P, 2, 6])
        mv1 = sb("mv1", [P, 2, 2])
        mv2 = sb("mv2", [P, 2, 2])
        ve1 = sb("ve1", [P, 2])
        ve2 = sb("ve2", [P, 2])
        rstd1 = sb("rstd1", [P, 2])
        rstd2 = sb("rstd2", [P, 2])
        smax = sb("smax", [P, 2, HALVES * DC])
        sbias = sb("sbias", [P, 2, HALVES * DC])
        ssum = sb("ssum", [P, 2, HALVES * DC])
        srec = sb("srec", [P, 2, HALVES * DC])
        lmax = sb("lmax", [P, 2])
        lbias = sb("lbias", [P, 2])
        lexp = sb("lexp", [P, 2, EXPERTS])
        lsum = sb("lsum", [P, 2])
        lrec = sb("lrec", [P, 2])
        p_all = sb("p_all", [P, 2, EXPERTS])
        p_top = sb("p_top", [P, 2, TOPK])
        p_topsum = sb("p_topsum", [P, 2])
        p_toprec = sb("p_toprec", [P, 2])
        p_marked = sb("p_marked", [P, 2, EXPERTS])
        chosen = sb("chosen", [P, 2, EXPERTS], F16)
        earlier = sb("earlier", [P, RING, EXPERTS], F16)
        kept = sb("kept", [P, 2, EXPERTS])
        place = sb("place", [P, 2, EXPERTS])
        placed = sb("placed", [P, 2, EXPERTS])
        dest = sb("dest", [P, 2, TOPK])
        dest_i = sb("dest_i", [P, 2, TOPK], I32)
        dest_slot = sb("dest_slot", [P, 2, TOPK], I32)
        dest_expert = sb("dest_expert", [P, 2, TOPK], I32)
        empty = sb("empty", [P, EXPERTS])
        index = sb("index", [P, EXPERTS], U32)

        flat_probs = probs[:, :, :].rearrange("p a f -> p (a f)")
        xe = flat_probs[:, 0:RING * ROW].rearrange("p (r f) -> p r f", r=RING)
        xeT = flat_probs[:, RING * ROW:RING * ROW + 2 * D].rearrange("p (a f) -> p a f", a=2)
        flat_tok = tok_sb[:, :, :].rearrange("p a f -> p (a f)")
        at = RING * D
        ye = flat_tok[:, 0:at].rearrange("p (r f) -> p r f", r=RING)
        sg = flat_tok[:, at:at + 2 * INNER].rearrange("p (a f) -> p a f", a=2)
        at += 2 * INNER
        h = flat_tok[:, at:at + 2 * INNER].rearrange("p (a f) -> p a f", a=2)
        at += 2 * INNER
        hT = flat_tok[0:INNER, at:at + 2 * P].rearrange("p (a f) -> p a f", a=2)
        zeros = wgu_sb[:, EXPERTS - 1, 0:ROW]
        flat_w = wgu_sb[:, :, :].rearrange("p e f -> p (e f)")
        span = TOKENS // P * D
        last = [flat_w[:, n * span:(n + 1) * span] for n in range(SUMS)]

        ps = ctx.enter_context(nc.psum_tensor("ps", [P, 8, 512], F32))

        def scores_ps(t2):
            return ps[:, 2 * t2:2 * t2 + 2, :]

        mix_ps = ps[:, 4, 0:D]
        index_ps = ps[:, 5, 0:EXPERTS]

        def xnT_ps(t2):
            return ps[:, 6 + t2, 0:D]

        def logits_ps(t2):
            return ps[:, 6 + t2, D:D + EXPERTS]

        def rank_ps(t2):
            return ps[:, 6 + t2, D + EXPERTS:D + 2 * EXPERTS]

        def xeT_ps(e2):
            return ps[:, e2, 0:D]

        def gu_ps(e2):
            return ps[:, 2 + e2, 0:2 * INNER]

        def hT_ps(e2):
            return ps[0:INNER, 4 + e2, 0:P]

        def ye_ps(e2):
            return ps[:, 6 + e2, 0:D]

        tok_loaded = [sem(f"tok_loaded{r}") for r in range(RING)]
        wr_loaded = sem("wr_loaded")
        weights_loaded = sem("weights_loaded")
        zeros_set = sem("zeros_set")
        zeros_stored = sem("zeros_stored")
        x1_stored = [sem(f"x1_stored{r}") for r in range(2)]
        row_stored = [sem(f"row_stored{r}") for r in range(RING)]
        const_step = sem("const_step")
        const_ready = sem("const_ready")
        stats1_ready, mv1_ready, ve1_ready, rstd1_ready, xn_ready = map(sem, (
            "stats1_ready", "mv1_ready", "ve1_ready", "rstd1_ready", "xn_ready"))
        scores_ready, smax_ready, sbias_ready, probs_ready, srec_ready, vT_ready = map(sem, (
            "scores_ready", "smax_ready", "sbias_ready", "probs_ready", "srec_ready", "vT_ready"))
        mix_ready, x1_ready = map(sem, ("mix_ready", "x1_ready"))
        stats2_ready, mv2_ready, ve2_ready, rstd2_ready, row_ready = map(sem, (
            "stats2_ready", "mv2_ready", "ve2_ready", "rstd2_ready", "row_ready"))
        xnT_ready, xnT_copied, logits_ready, lmax_ready, lbias_ready, lexp_ready = map(sem, (
            "xnT_ready", "xnT_copied", "logits_ready", "lmax_ready", "lbias_ready", "lexp_ready"))
        lrec_ready, p_ready, top_ready, topsum_ready, toprec_ready, marked_ready, chosen_ready = map(sem, (
            "lrec_ready", "p_ready", "top_ready", "topsum_ready", "toprec_ready", "marked_ready", "chosen_ready"))
        shares_ready, earlier_ready, rank_ready = map(sem, ("shares_ready", "earlier_ready", "rank_ready"))
        kept_ready, place_ready, placed_ready, dest_ready, dest_i_ready, dest_split = map(sem, (
            "kept_ready", "place_ready", "placed_ready", "dest_ready", "dest_i_ready", "dest_split"))
        token_now_ready, expert_hot_ready, slot_hot_ready, index_summed = map(sem, (
            "token_now_ready", "expert_hot_ready", "slot_hot_ready", "index_summed"))
        empty_ready, index_ready = map(sem, ("empty_ready", "index_ready"))
        gathered = [sem(f"gathered{r}") for r in range(RING)]
        scattered = [sem(f"scattered{n}") for n in range(SUMS)]
        xeT_ready, xeT_copied, gu_ready, sg_ready, h_ready = map(sem, (
            "xeT_ready", "xeT_copied", "gu_ready", "sg_ready", "h_ready"))
        hT_ready, hT_copied, ye_ready, ye_copied = map(sem, ("hT_ready", "hT_copied", "ye_ready", "ye_copied"))
        LAST = 4
        last_loaded = [sem(f"last_loaded{c}") for c in range(LAST)]
        last_added = sem("last_added")
        out_stored = sem("out_stored")

        block = ctx.enter_context(nc.Block())

        def run(eng, slots, total, step):
            def ok_at(s):
                return lambda lag: 0 <= s - lag < slots

            peel = 2 * UNROLL
            for s in range(peel):
                step(s, s % UNROLL, ok_at(s))
            with eng.Fori(peel, slots - UNROLL + 1, UNROLL) as base:
                for u in range(UNROLL):
                    step(base + u, u, lambda lag: True)
            for s in range(slots, total):
                step(s, s % UNROLL, ok_at(s))

        def reused(eng, semaphore, i, ring, per=1):
            if not isinstance(i, int) or i >= ring:
                eng.wait_ge(semaphore, per * (i - ring + 1))

        def dma_reused(eng, semaphores, i, r, ring):
            if not isinstance(i, int) or i >= ring:
                eng.wait_ge(semaphores[r], 16 * ((i - r) // ring) if isinstance(i, int)
                            else (i - r) * (16 // ring))

        @block.sync
        def _(sp):
            def load(t, r):
                sp.dma_start(tok_sb[:, r, :], tok[bass.ds(t * P, P), :]).then_inc(tok_loaded[r], 16)

            def keep(t, r):
                sp.wait_ge(x1_ready, t + 1)
                sp.dma_start(sums[0][bass.ds(t * P, P), :], x1[:, r % 2, :]).then_inc(x1_stored[r % 2], 16)

            def publish(t, r):
                sp.wait_ge(shares_ready, t + 1)
                sp.wait_ge(row_ready, t + 1)
                sp.dma_start(table[bass.ds(t * P, P), :], row[:, r, :]).then_inc(row_stored[r], 16)

            def weights(g):
                sp.dma_start(wgu_sb[:, bass.ds(g * GROUP, GROUP), :],
                             wgu[:, bass.ds(g * GROUP, GROUP), :]).then_inc(weights_loaded, 16)
                sp.dma_start(wd_sb[:, bass.ds(g * GROUP, GROUP), :],
                             wd[:, bass.ds(g * GROUP, GROUP), :]).then_inc(weights_loaded, 16)

            for t in range(RING):
                load(t, t)
            sp.dma_start(wr_sb[:, :, :], wr).then_inc(wr_loaded, 16)
            sp.wait_ge(zeros_set, 1)
            sp.dma_start(table[TOKENS:TOKENS + P, :], zeros).then_inc(zeros_stored, 16)
            sp.dma_start(sums[0][TOKENS:TOKENS + P, :], zeros[:, 0:D]).then_inc(zeros_stored, 16)
            for n in range(1, SUMS):
                sp.dma_start(sums[n].rearrange("(a p) d -> p a d", p=P),
                             zeros[:, 0:D].unsqueeze(1).broadcast_to([P, TOKENS // P + 1, D])
                             ).then_inc(zeros_stored, 16)

            def step(t, r, more):
                keep(t, r)
                if more:
                    load(t + RING, r)
                if not isinstance(t, int) or t >= 1:
                    publish(t - 1, (r - 1) % RING)

            for t in range(RING):
                step(t, t, True)
            sp.wait_ge(zeros_stored, 16 * (SUMS + 1))
            with sp.Fori(RING, TILES - RING - UNROLL + 1, UNROLL) as base:
                for u in range(UNROLL):
                    step(base + u, u, True)
                    weights(base + u - RING)
            for t in range(TILES - RING, TILES):
                step(t, t % RING, False)
            publish(TILES - 1, (TILES - 1) % RING)

            sp_last = [s.rearrange("(p a) d -> p (a d)", p=P) for s in (a[0:TOKENS, :] for a in sums)]
            out_view = out_rows.rearrange("(p a) d -> p (a d)", p=P)
            w = span // LAST
            for n in range(SUMS):
                sp.wait_ge(scattered[n], 16 * (EXPERTS // SUMS))
            for c in range(LAST):
                for n in range(SUMS):
                    sp.dma_start(last[n][:, c * w:(c + 1) * w], sp_last[n][:, c * w:(c + 1) * w]
                                 ).then_inc(last_loaded[c], 16)
            for c in range(LAST):
                sp.wait_ge(last_added, c + 1)
                sp.dma_start(out_view[:, c * w:(c + 1) * w], last[0][:, c * w:(c + 1) * w]).then_inc(out_stored, 16)
            sp.wait_ge(out_stored, 16 * LAST)

        @block.gpsimd
        def _(pool):
            pool.memset(ident[:, :], 0.0).then_inc(const_step, 1)
            pool.memset(before[:, :], 1.0).then_inc(const_step, 1)
            pool.iota(count_i[:, :], [[1, P]], base=0, channel_multiplier=0).then_inc(const_step, 1)
            pool.iota(spare_i[:, :], [[0, 1]], base=TOKENS + 1, channel_multiplier=1).then_inc(const_step, 1)
            pool.memset(eps[:, :], EPS).then_inc(const_ready, 1)
            pool.memset(neg_half[:, :], -0.5).then_inc(const_ready, 1)
            pool.memset(ones[:, :], 1.0).then_inc(const_ready, 1)
            pool.memset(earlier[:, 0, :], 0.0).then_inc(const_ready, 1)
            pool.iota(token_no[:, :], [[P, TILES]], base=1, channel_multiplier=1).then_inc(const_ready, 1)
            pool.wait_ge(const_step, 4)
            pool.affine_select(out=ident[:, :], in_=ident[:, :], compare_op=ALU.not_equal, fill=1.0, base=0,
                               pattern=[[-1, P]], channel_multiplier=1).then_inc(const_ready, 1)
            pool.affine_select(out=before[:, :], in_=before[:, :], compare_op=ALU.is_ge, fill=0.0, base=-1,
                               pattern=[[1, P]], channel_multiplier=-1).then_inc(const_ready, 1)
            pool.tensor_copy(count[:, :], count_i[:, :]).then_inc(const_ready, 1)
            pool.tensor_scalar(expert_base[:, :], count_i[:, 0:EXPERTS], float(CAP), 1.0, ALU.mult, ALU.add
                               ).then_inc(const_ready, 1)
            pool.tensor_copy(spare[:, :], spare_i[:, :]).then_inc(const_ready, 1)
            pool.wait_ge(const_ready, CONSTS)

            def rstd(t, a, mv_ready, mv, ve_ready, ve, rstd_ready, out_):
                pool.wait_ge(mv_ready, t + 1)
                pool.tensor_add(ve[:, a:a + 1], mv[:, a, 1:2], eps[:, :]).then_inc(ve_ready, 1)
                pool.wait_ge(ve_ready, t + 1)
                pool.tensor_tensor(out_[:, a:a + 1], ve[:, a:a + 1], neg_half[:, :], ALU.pow).then_inc(rstd_ready, 1)

            def experts(t, a):
                pool.tensor_copy(token_now[:, a:a + 1], token_no[:, bass.ds(t, 1)]).then_inc(token_now_ready, 1)
                pool.wait_ge(token_now_ready, t + 1)
                pool.wait_ge(dest_split, 2 * (t + 1))
                reused(pool, index_summed, t, 2)
                for k in range(TOPK):
                    pool.tensor_scalar(expert_hot[:, a, k, :], count[:, 0:EXPERTS], dest_expert[:, a, k:k + 1],
                                       token_now[:, a:a + 1], ALU.is_equal, ALU.mult).then_inc(expert_hot_ready, 1)

            rstd(0, 0, mv1_ready, mv1, ve1_ready, ve1, rstd1_ready, rstd1)

            def step(s, u, ok):
                if ok(-1):
                    rstd(s + 1, (u + 1) % 2, mv1_ready, mv1, ve1_ready, ve1, rstd1_ready, rstd1)
                if ok(1):
                    rstd(s - 1, (u - 1) % 2, mv2_ready, mv2, ve2_ready, ve2, rstd2_ready, rstd2)
                if ok(3):
                    experts(s - 3, (u - 3) % 2)

            steps(pool, step)

            def gather(e):
                if e >= RING:
                    pool.wait_ge(h_ready, e - RING + 1)
                pool.indirect_dma_start(xe[:, e % RING, :], None, table,
                                        bass.IndirectOffsetOnAxis(ap=index[:, e:e + 1], axis=0)
                                        ).then_inc(gathered[e % RING], 16)

            def scatter(e):
                pool.wait_ge(ye_copied, e + 1)
                if e >= SUMS:
                    pool.wait_ge(scattered[e % SUMS], 16 * (e // SUMS))
                pool.indirect_dma_start(sums[e % SUMS], bass.IndirectOffsetOnAxis(ap=index[:, e:e + 1], axis=0),
                                        ye[:, e % RING, :], None, compute_op=ALU.add
                                        ).then_inc(scattered[e % SUMS], 16)

            pool.wait_ge(index_ready, 1)
            pool.wait_ge(zeros_stored, 16 * (SUMS + 1))
            for r in range(RING):
                pool.wait_ge(row_stored[r], 16 * (TILES // RING))
                pool.wait_ge(x1_stored[r % 2], 16 * (TILES // 2))
            gather(0)
            gather(1)
            for e in range(EXPERTS):
                if e + 2 < EXPERTS:
                    gather(e + 2)
                if e >= 3:
                    scatter(e - 3)
            for e in range(EXPERTS - 3, EXPERTS):
                scatter(e)
            for n in range(SUMS):
                pool.wait_ge(scattered[n], 16 * (EXPERTS // SUMS))

        @block.vector
        def _(dve):
            dve.memset(zeros, 0.0).then_inc(zeros_set, 1)

            def norm1_stats(t, u):
                a, r = u % 2, u % RING
                dve.wait_ge(tok_loaded[r], 16 * (t // RING + 1) if isinstance(t, int) else (t - r) * (16 // RING) + 16)
                dve.bn_stats(stats1[:, a, :], tok_sb[:, r, 0:D]).then_inc(stats1_ready, 1)
                dve.wait_ge(stats1_ready, t + 1)
                dve.bn_aggr(mv1[:, a, :], stats1[:, a, :]).then_inc(mv1_ready, 1)

            def norm1(t, u):
                a, r = u % 2, u % RING
                dve.wait_ge(rstd1_ready, t + 1)
                dve.wait_ge(mv1_ready, t + 1)
                reused(dve, scores_ready, t, 2)
                dve.tensor_scalar(xn[:, a, :], tok_sb[:, r, 0:D], mv1[:, a, 0:1], rstd1[:, a:a + 1],
                                  ALU.subtract, ALU.mult).then_inc(xn_ready, 1)

            def score_max(t, u):
                a = u % 2
                dve.wait_ge(scores_ready, t + 1)
                dve.reduce_max(smax[:, a, :], scores_ps(a).rearrange("p b (c d) -> p (b c) d", c=DC), axis=AX.X
                               ).then_inc(smax_ready, 1)
                dve.wait_ge(smax_ready, t + 1)
                reused(dve, probs_ready, t, 2, HALVES * DC)
                dve.tensor_scalar(sbias[:, a, :], smax[:, a, :], -SCALE, None, ALU.mult).then_inc(sbias_ready, 1)

            def values(t, u):
                a, r = u % 2, u % RING
                dve.wait_ge(probs_ready, HALVES * DC * (t + 1))
                dve.reciprocal(srec[:, a, :], ssum[:, a, :]).then_inc(srec_ready, 1)
                dve.wait_ge(srec_ready, t + 1)
                reused(dve, mix_ready, t, 2)
                dve.tensor_tensor(vT[:, a, :].rearrange("p (n s) -> p n s", s=SEQ),
                                  tok_sb[:, r, 2 * D:3 * D].rearrange("p (n s) -> p n s", s=SEQ),
                                  srec[:, a, :].unsqueeze(2).broadcast_to([P, HALVES * DC, SEQ]), ALU.mult
                                  ).then_inc(vT_ready, 1)

            def residual(t, u):
                a, r = u % 2, u % RING
                dve.wait_ge(mix_ready, t + 1)
                dma_reused(dve, x1_stored, t, a, 2)
                dve.tensor_tensor(x1[:, a, :], mix_ps, tok_sb[:, r, 0:D], ALU.add).then_inc(x1_ready, 1)
                dve.wait_ge(x1_ready, t + 1)
                dve.bn_stats(stats2[:, a, :], x1[:, a, :]).then_inc(stats2_ready, 1)
                dve.wait_ge(stats2_ready, t + 1)
                dve.bn_aggr(mv2[:, a, :], stats2[:, a, :]).then_inc(mv2_ready, 1)

            def norm2(t, u):
                a, r = u % 2, u % RING
                dve.wait_ge(rstd2_ready, t + 1)
                dve.wait_ge(mv2_ready, t + 1)
                dma_reused(dve, row_stored, t, r, RING)
                dve.tensor_scalar(row[:, r, 0:D], x1[:, a, :], mv2[:, a, 0:1], rstd2[:, a:a + 1],
                                  ALU.subtract, ALU.mult).then_inc(row_ready, 1)

            def logit_max(t, u):
                a = u % 2
                dve.wait_ge(logits_ready, t + 1)
                dve.reduce_max(lmax[:, a:a + 1], logits_ps(a), axis=AX.X).then_inc(lmax_ready, 1)
                dve.wait_ge(lmax_ready, t + 1)
                dve.tensor_scalar(lbias[:, a:a + 1], lmax[:, a:a + 1], -1.0, None, ALU.mult).then_inc(lbias_ready, 1)

            def choose(t, u):
                a, r = u % 2, u % RING
                dve.wait_ge(lexp_ready, t + 1)
                dve.reciprocal(lrec[:, a:a + 1], lsum[:, a:a + 1]).then_inc(lrec_ready, 1)
                dve.wait_ge(lrec_ready, t + 1)
                dve.tensor_scalar(p_all[:, a, :], lexp[:, a, :], lrec[:, a:a + 1], None, ALU.mult).then_inc(p_ready, 1)
                dve.wait_ge(p_ready, t + 1)
                dve.max(p_top[:, a, :], p_all[:, a, :]).then_inc(top_ready, 1)
                dve.wait_ge(top_ready, t + 1)
                dve.match_replace(p_marked[:, a, :], p_top[:, a, :], p_all[:, a, :], -1.0).then_inc(marked_ready, 1)
                dve.reduce_sum(p_topsum[:, a:a + 1], p_top[:, a, :], axis=AX.X).then_inc(topsum_ready, 1)
                dve.wait_ge(marked_ready, t + 1)
                reused(dve, rank_ready, t, 2)
                dve.tensor_scalar(chosen[:, a, :], p_marked[:, a, :], 0.0, None, ALU.is_lt).then_inc(chosen_ready, 1)
                dve.wait_ge(topsum_ready, t + 1)
                dve.reciprocal(p_toprec[:, a:a + 1], p_topsum[:, a:a + 1]).then_inc(toprec_ready, 1)
                dve.wait_ge(chosen_ready, t + 1)
                reused(dve, rank_ready, t, RING - 1)
                if not isinstance(t, int) or t >= 1:
                    dve.wait_ge(earlier_ready, t)
                dve.tensor_tensor(earlier[:, (r + 1) % RING, :], earlier[:, r, :], chosen[:, a, :], ALU.add
                                  ).then_inc(earlier_ready, 1)
                dve.wait_ge(toprec_ready, t + 1)
                dve.scalar_tensor_tensor(row[:, r, D:ROW], p_all[:, a, :], p_toprec[:, a:a + 1], chosen[:, a, :],
                                         ALU.mult, ALU.mult).then_inc(shares_ready, 1)

            def places(t, u):
                a = u % 2
                dve.wait_ge(rank_ready, t + 1)
                dve.scalar_tensor_tensor(kept[:, a, :], rank_ps(a), float(CAP), chosen[:, a, :], ALU.is_lt, ALU.mult
                                         ).then_inc(kept_ready, 1)
                dve.tensor_tensor(place[:, a, :], rank_ps(a), expert_base[:, :], ALU.add).then_inc(place_ready, 1)
                dve.wait_ge(kept_ready, t + 1)
                dve.wait_ge(place_ready, t + 1)
                dve.tensor_tensor(placed[:, a, :], place[:, a, :], kept[:, a, :], ALU.mult).then_inc(placed_ready, 1)
                dve.wait_ge(placed_ready, t + 1)
                dve.max(dest[:, a, :], placed[:, a, :]).then_inc(dest_ready, 1)
                dve.wait_ge(dest_ready, t + 1)
                dve.tensor_scalar(dest_i[:, a, :], dest[:, a, :], -1.0, None, ALU.add).then_inc(dest_i_ready, 1)
                dve.wait_ge(dest_i_ready, t + 1)
                reused(dve, expert_hot_ready, t, 2, TOPK)
                dve.tensor_scalar(dest_expert[:, a, :], dest_i[:, a, :], CAP_BITS, None, ALU.arith_shift_right
                                  ).then_inc(dest_split, 1)
                dve.tensor_scalar(dest_slot[:, a, :], dest_i[:, a, :], CAP - 1, None, ALU.bitwise_and
                                  ).then_inc(dest_split, 1)

            def slots_hot(t, u):
                a = u % 2
                dve.wait_ge(dest_split, 2 * (t + 1))
                reused(dve, index_summed, t, 2)
                for k in range(TOPK):
                    dve.tensor_scalar(slot_hot[:, a, k, :], count[:, 0:CAP], dest_slot[:, a, k:k + 1], None,
                                      ALU.is_equal).then_inc(slot_hot_ready, 1)

            norm1_stats(0, 0)
            norm1(0, 0)
            dve.wait_ge(const_ready, CONSTS)

            def step(s, u, ok):
                if ok(-1):
                    norm1_stats(s + 1, u + 1)
                if ok(0):
                    score_max(s, u)
                if ok(3):
                    places(s - 3, u - 3)
                if ok(1):
                    residual(s - 1, u - 1)
                if ok(2):
                    logit_max(s - 2, u - 2)
                if ok(3):
                    slots_hot(s - 3, u - 3)
                if ok(1):
                    norm2(s - 1, u - 1)
                if ok(-1):
                    norm1(s + 1, u + 1)
                if ok(0):
                    values(s, u)
                if ok(2):
                    choose(s - 2, u - 2)

            steps(dve, step)

            dve.wait_ge(index_summed, TILES)
            dve.tensor_scalar(empty[:, :], index_ps, 0.0, spare[:, 0:1], ALU.is_equal, ALU.mult).then_inc(empty_ready, 1)
            dve.wait_ge(empty_ready, 1)
            dve.scalar_tensor_tensor(index[:, :], index_ps, -1.0, empty[:, :], ALU.add, ALU.add
                                     ).then_inc(index_ready, 1)

            def step_e(s, u, ok):
                if ok(1):
                    e, a, r = s - 1, (u - 1) % 2, (u - 1) % RING
                    dve.wait_ge(sg_ready, e + 1)
                    reused(dve, hT_ready, e, 2)
                    dve.scalar_tensor_tensor(h[:, a, :], gu_ps(a)[:, INNER:2 * INNER],
                                             xe[:, r, bass.ds(e + D, 1)], sg[:, a, :], ALU.mult, ALU.mult
                                             ).then_inc(h_ready, 1)
                if ok(2):
                    e, a = s - 2, (u - 2) % 2
                    dve.wait_ge(hT_ready, e + 1)
                    reused(dve, ye_ready, e, 2)
                    dve.tensor_copy(hT[:, a, :], hT_ps(a)).then_inc(hT_copied, 1)

            run(dve, EXPERTS, EXPERTS + 3, step_e)

            w = span // LAST
            for c in range(LAST):
                dve.wait_ge(last_loaded[c], 16 * SUMS)
                dve.tensor_tensor(last[0][:, c * w:(c + 1) * w], last[0][:, c * w:(c + 1) * w],
                                  last[1][:, c * w:(c + 1) * w], ALU.add).then_inc(last_added, 1)

        @block.scalar
        def _(act):
            def soften(t, u):
                a = u % 2
                act.wait_ge(sbias_ready, t + 1)
                reused(act, mix_ready, t, 2)
                reused(act, srec_ready, t, 2)
                for n in range(HALVES * DC):
                    act.activation(probs[:, a, n * D:(n + 1) * D], scores_ps(a)[:, n // DC, (n % DC) * D:(n % DC + 1) * D],
                                   ACT.Exp, bias=sbias[:, a, n:n + 1], scale=SCALE, accum_out=ssum[:, a, n:n + 1]
                                   ).then_inc(probs_ready, 1)

            def copy_xnT(t, u):
                a = u % 2
                act.wait_ge(xnT_ready, t + 1)
                reused(act, logits_ready, t, 2)
                act.activation(xnT[:, a, :], xnT_ps(a), ACT.Copy).then_inc(xnT_copied, 1)

            def logit_exp(t, u):
                a = u % 2
                act.wait_ge(lbias_ready, t + 1)
                reused(act, p_ready, t, 2)
                act.activation(lexp[:, a, :], logits_ps(a), ACT.Exp, bias=lbias[:, a:a + 1],
                               accum_out=lsum[:, a:a + 1]).then_inc(lexp_ready, 1)

            def step(s, u, ok):
                if ok(2):
                    copy_xnT(s - 2, u - 2)
                if ok(0):
                    soften(s, u)
                if ok(2):
                    logit_exp(s - 2, u - 2)

            steps(act, step)

            def step_e(s, u, ok):
                if ok(0):
                    e, a = s, u % 2
                    act.wait_ge(xeT_ready, e + 1)
                    reused(act, gu_ready, e, 2)
                    act.activation(xeT[:, a, :], xeT_ps(a), ACT.Copy).then_inc(xeT_copied, 1)
                if ok(1):
                    e, a = s - 1, (u - 1) % 2
                    act.wait_ge(gu_ready, e + 1)
                    reused(act, h_ready, e, 2)
                    act.activation(sg[:, a, :], gu_ps(a)[:, 0:INNER], ACT.Silu).then_inc(sg_ready, 1)
                if ok(3):
                    e, a, r = s - 3, (u - 3) % 2, (u - 3) % RING
                    act.wait_ge(ye_ready, e + 1)
                    if not isinstance(e, int) or e >= RING:
                        act.wait_ge(scattered[a], ((e - RING) // SUMS + 1) * 16 if isinstance(e, int)
                                    else (e - RING - a) * (16 // SUMS) + 16)
                    act.activation(ye[:, r, :], ye_ps(a), ACT.Copy).then_inc(ye_copied, 1)

            run(act, EXPERTS, EXPERTS + 3, step_e)

        @block.tensor
        def _(pe):
            pe.wait_ge(const_ready, CONSTS)
            pe.wait_ge(wr_loaded, 16)

            def scores(t, u):
                a, r = u % 2, u % RING
                pe.wait_ge(xn_ready, t + 1)
                reused(pe, probs_ready, t, 2, HALVES * DC)
                for c in range(DC):
                    for b in range(HALVES):
                        rows = slice(b * SEQ, (b + 1) * SEQ)
                        mm = pe.matmul(scores_ps(a)[:, b, c * D:(c + 1) * D],
                                       tok_sb[rows, r, D + c * P:D + (c + 1) * P], xn[rows, a, :], start=True, stop=True)
                mm.then_inc(scores_ready, 1)

            def mix(t, u):
                a = u % 2
                pe.wait_ge(vT_ready, t + 1)
                if not isinstance(t, int) or t >= 1:
                    pe.wait_ge(x1_ready, t)
                for c in range(DC):
                    for b in range(HALVES):
                        n = b * DC + c
                        mm = pe.matmul(mix_ps[b * SEQ:(b + 1) * SEQ, :], vT[:, a, n * SEQ:(n + 1) * SEQ],
                                       probs[:, a, n * D:(n + 1) * D], start=(c == 0), stop=(c == DC - 1))
                mm.then_inc(mix_ready, 1)

            def turn(t, u):
                a, r = u % 2, u % RING
                pe.wait_ge(row_ready, t + 1)
                reused(pe, place_ready, t, 2)
                reused(pe, kept_ready, t, 2)
                for c in range(DC):
                    mm = pe.transpose(xnT_ps(a)[:, c * P:(c + 1) * P], row[:, r, c * P:(c + 1) * P], ident[:, :])
                mm.then_inc(xnT_ready, 1)

            def logits(t, u):
                a = u % 2
                pe.wait_ge(xnT_copied, t + 1)
                for c in range(DC):
                    mm = pe.matmul(logits_ps(a), xnT[:, a, c * P:(c + 1) * P], wr_sb[:, c, :],
                                   start=(c == 0), stop=(c == DC - 1))
                mm.then_inc(logits_ready, 1)

            def rank(t, u):
                a, r = u % 2, u % RING
                pe.wait_ge(chosen_ready, t + 1)
                if not isinstance(t, int) or t >= 1:
                    pe.wait_ge(earlier_ready, t)
                pe.matmul(rank_ps(a), before[:, :], chosen[:, a, :], start=True, stop=False)
                pe.matmul(rank_ps(a), ones[:, :], earlier[:, r, :], start=False, stop=True).then_inc(rank_ready, 1)

            def index_add(t, u):
                a = u % 2
                pe.wait_ge(slot_hot_ready, TOPK * (t + 1))
                pe.wait_ge(expert_hot_ready, TOPK * (t + 1))
                first = isinstance(t, int) and t == 0
                for k in range(TOPK):
                    mm = pe.matmul(index_ps, slot_hot[:, a, k, :], expert_hot[:, a, k, :],
                                   start=(first and k == 0),
                                   stop=(isinstance(t, int) and t == TILES - 1 and k == TOPK - 1))
                mm.then_inc(index_summed, 1)

            def step(s, u, ok):
                if ok(2):
                    turn(s - 2, u - 2)
                if ok(0):
                    scores(s, u)
                if ok(3):
                    rank(s - 3, u - 3)
                if ok(2):
                    logits(s - 2, u - 2)
                if ok(1):
                    mix(s - 1, u - 1)
                if ok(4):
                    index_add(s - 4, u - 4)

            steps(pe, step)

            pe.wait_ge(weights_loaded, 16 * 2 * GROUPS)

            def step_e(s, u, ok):
                if ok(0):
                    e, a, r = s, u % 2, u % RING
                    pe.wait_ge(gathered[r], 16 * (e // RING + 1) if isinstance(e, int) else (e - r) * (16 // RING) + 16)
                    reused(pe, xeT_copied, e, 2)
                    for c in range(DC):
                        mm = pe.transpose(xeT_ps(a)[:, c * P:(c + 1) * P], xe[:, r, c * P:(c + 1) * P], ident[:, :])
                    mm.then_inc(xeT_ready, 1)
                if ok(2):
                    e, a = s - 2, (u - 2) % 2
                    pe.wait_ge(h_ready, e + 1)
                    reused(pe, hT_copied, e, 2)
                    pe.transpose(hT_ps(a), h[:, a, :], ident[:, :]).then_inc(hT_ready, 1)
                if ok(1):
                    e, a = s - 1, (u - 1) % 2
                    pe.wait_ge(xeT_copied, e + 1)
                    reused(pe, h_ready, e, 2)
                    for c in range(DC):
                        mm = pe.matmul(gu_ps(a), xeT[:, a, c * P:(c + 1) * P],
                                       wgu_sb[:, bass.ds(e, 1), c * 2 * INNER:(c + 1) * 2 * INNER],
                                       start=(c == 0), stop=(c == DC - 1))
                    mm.then_inc(gu_ready, 1)
                if ok(3):
                    e, a = s - 3, (u - 3) % 2
                    pe.wait_ge(hT_copied, e + 1)
                    reused(pe, ye_copied, e, 2)
                    pe.matmul(ye_ps(a), hT[:, a, :], wd_sb[:, bass.ds(e, 1), :], start=True, stop=True
                              ).then_inc(ye_ready, 1)

            run(pe, EXPERTS, EXPERTS + 3, step_e)


CONSTS = 10
CAP_BITS = CAP.bit_length() - 1
SCALE = float(D) ** -0.5


def steps(eng, step):
    peel = 2 * UNROLL
    turn = TILES - UNROLL

    def ok_at(s):
        return lambda lag: 0 <= s - lag < TILES

    for s in range(peel):
        step(s, s, ok_at(s))
    with eng.Fori(peel, turn - UNROLL + 1, UNROLL) as base:
        for u in range(UNROLL):
            step(base + u, peel + u, lambda lag: True)
    for s in range(turn, TILES + 4):
        step(s, s, ok_at(s))


def kernel(**inputs):
    import concourse.bacc as _bacc
    from concourse.bass_utils import run_bass_kernel_spmd as _run

    x = np.asarray(inputs["x"]).reshape(TOKENS, D)
    c = np.asarray(inputs["ctx_2048"])
    cT = c.reshape(TILES, HALVES, SEQ, DC, P).transpose(0, 4, 1, 3, 2).reshape(TOKENS, D)
    gate, up = (np.asarray(inputs[n]).reshape(EXPERTS, DC, P, INNER) for n in ("L0_ffn_gate_proj", "L0_ffn_up_proj"))
    arrays = {
        "tok": np.concatenate([x, c.reshape(TOKENS, D), cT], axis=1),
        "wgu": np.stack([gate, up], axis=3).transpose(2, 0, 1, 3, 4).reshape(P, EXPERTS, DC * 2 * INNER),
        "wd": np.asarray(inputs["L0_ffn_down_proj"]).transpose(1, 0, 2),
        "wr": np.asarray(inputs["L0_ffn_router_weight"]).reshape(DC, P, EXPERTS).transpose(1, 0, 2),
    }
    arrays = {k: np.ascontiguousarray(v) for k, v in arrays.items()}
    nc = _bacc.Bacc("TRN2", target_bir_lowering=False, num_devices=1)
    args = [nc.dram_tensor(f"in_{k}", v.shape, F32, kind="ExternalInput").ap() for k, v in arrays.items()]
    out = nc.dram_tensor("out_x", (BATCH, SEQ, D), F32, kind="ExternalOutput").ap()
    build(nc, *args, out)
    r = _run(nc, [{f"in_{k}": v for k, v in arrays.items()}], core_ids=[0])
    return r.results[0]["out_x"]
```

```python
from contextlib import ExitStack

import numpy as np

import concourse.bass as bass
from concourse import mybir

P = 128
BATCH, SEQ, D = 32, 64, 256
TOKENS = BATCH * SEQ
TILES = TOKENS // P
HALVES = P // SEQ
DC = D // P
EXPERTS, INNER, TOPK = 64, 96, 8
CAP = 2 * (512 * TOPK) // EXPERTS
ROW = D + EXPERTS
UNROLL = 4
RING = 4
SUMS = 2
GROUP = 8
GROUPS = EXPERTS // GROUP
EPS = 1e-5
KEY = TOKENS

F32 = mybir.dt.float32
F16 = mybir.dt.float16
I32 = mybir.dt.int32
U32 = mybir.dt.uint32
ALU = mybir.AluOpType
ACT = mybir.ActivationFunctionType
AX = mybir.AxisListType


def build(nc, tok, wgu, wd, wr, out):
    table = nc.dram_tensor("table", [TOKENS + P, ROW], F32, kind="Internal").ap()
    sums = [nc.dram_tensor(f"sum{n}", [TOKENS + P, D], F32, kind="Internal").ap() for n in range(SUMS)]
    out_rows = out.rearrange("b s d -> (b s) d")

    with ExitStack() as ctx:
        def sb(name, shape, dt=F32):
            return ctx.enter_context(nc.sbuf_tensor(name, shape, dt))

        def sem(name):
            return ctx.enter_context(nc.semaphore(name))

        wgu_sb = sb("wgu_sb", [P, EXPERTS, DC * 2 * INNER])
        wd_sb = sb("wd_sb", [INNER, EXPERTS, D])
        wr_sb = sb("wr_sb", [P, DC, EXPERTS])
        tok_sb = sb("tok_sb", [P, RING, 3 * D])
        xn = sb("xn", [P, 2, D])
        probs = sb("probs", [P, 2, HALVES * DC * D])
        vT = sb("vT", [P, 2, HALVES * DC * SEQ])
        x1 = sb("x1", [P, 2, D])
        row = sb("row", [P, RING, ROW])
        xnT = sb("xnT", [P, 2, D])
        slot_hot = sb("slot_hot", [P, 2, CAP, TOPK], F16)
        expert_hot = sb("expert_hot", [P, EXPERTS, TOPK], F16)
        expert_tok = sb("expert_tok", [P, EXPERTS, TOPK], F16)
        ident = sb("ident", [P, P])
        before = sb("before", [P, P], F16)
        ones = sb("ones", [P, P], F16)
        slot_no = sb("slot_no", [P, CAP, TOPK], F16)
        expert_no = sb("expert_no", [P, EXPERTS, TOPK], F16)
        expert_key = sb("expert_key", [P, EXPERTS], F16)
        token_no = sb("token_no", [P, TILES])
        spare = sb("spare", [P, 1])
        neg_half = sb("neg_half", [P, 1])
        stats1 = sb("stats1", [P, 2, 6])
        stats2 = sb("stats2", [P, 2, 6])
        mv1 = sb("mv1", [P, 2, 2])
        mv2 = sb("mv2", [P, 2, 2])
        ve1 = sb("ve1", [P, 2])
        ve2 = sb("ve2", [P, 2])
        rstd1 = sb("rstd1", [P, 2])
        rstd2 = sb("rstd2", [P, 2])
        sbias = sb("sbias", [P, 2, HALVES * DC])
        ssum = sb("ssum", [P, 2, HALVES * DC])
        srec = sb("srec", [P, 2, HALVES * DC])
        lbias = sb("lbias", [P, 2])
        lexp = sb("lexp", [P, 2, EXPERTS])
        lsum = sb("lsum", [P, 2])
        lrec = sb("lrec", [P, 2])
        p_all = sb("p_all", [P, 2, EXPERTS])
        p_top = sb("p_top", [P, 2, TOPK])
        p_topsum = sb("p_topsum", [P, 2])
        p_toprec = sb("p_toprec", [P, 2])
        p_marked = sb("p_marked", [P, 2, EXPERTS])
        chosen = sb("chosen", [P, 2, EXPERTS], F16)
        earlier = sb("earlier", [P, RING, EXPERTS], F16)
        placed = sb("placed", [P, 2, EXPERTS])
        dest = sb("dest", [P, 2, TOPK], I32)
        dest_parts = sb("dest_parts", [P, 2, 2, TOPK], I32)
        dest_half = sb("dest_half", [P, 2, 2, TOPK], F16)
        shift1 = sb("shift1", [P, 2])
        shift2 = sb("shift2", [P, 2])
        index = sb("index", [P, EXPERTS], U32)

        flat_probs = probs[:, :, :].rearrange("p a f -> p (a f)")
        xe = flat_probs[:, 0:RING * ROW].rearrange("p (r f) -> p r f", r=RING)
        xeT = flat_probs[:, RING * ROW:RING * ROW + 2 * D].rearrange("p (a f) -> p a f", a=2)
        flat_tok = tok_sb[:, :, :].rearrange("p a f -> p (a f)")
        at = RING * D
        empty = placed[:, 0, :]
        ye = flat_tok[:, 0:at].rearrange("p (r f) -> p r f", r=RING)
        sg = flat_tok[:, at:at + 2 * INNER].rearrange("p (a f) -> p a f", a=2)
        at += 2 * INNER
        h = flat_tok[:, at:at + 2 * INNER].rearrange("p (a f) -> p a f", a=2)
        at += 2 * INNER
        hT = flat_tok[0:INNER, at:at + 2 * P].rearrange("p (a f) -> p a f", a=2)
        zeros = wgu_sb[:, EXPERTS - 1, 0:ROW]
        def pattern_i(n, width):
            lane = wgu_sb[:, EXPERTS - 2 * GROUP + 3 * n:EXPERTS - 2 * GROUP + 3 * n + 3, :]
            return lane.rearrange("p e f -> p (e f)")[:, 0:width].bitcast(I32)

        flat_w = wgu_sb[:, :, :].rearrange("p e f -> p (e f)")
        span = TOKENS // P * D
        last = [flat_w[:, n * span:(n + 1) * span] for n in range(SUMS)]

        ps = ctx.enter_context(nc.psum_tensor("ps", [P, 8, 512], F32))

        def scores_ps(t2):
            return ps[:, 2 * t2:2 * t2 + 2, :]

        mix_ps = ps[:, 4, 0:D]
        index_ps = ps[:, 5, 0:EXPERTS]

        def xnT_ps(t2):
            return ps[:, 6 + t2, 0:D]

        def logits_ps(t2):
            return ps[:, 6 + t2, D:D + EXPERTS]

        def rank_ps(t2):
            return ps[:, 6 + t2, D + EXPERTS:D + 2 * EXPERTS]

        def xeT_ps(e2):
            return ps[:, e2, 0:D]

        def gu_ps(e2):
            return ps[:, 2 + e2, 0:2 * INNER]

        def hT_ps(e2):
            return ps[0:INNER, 4 + e2, 0:P]

        def ye_ps(e2):
            return ps[:, 6 + e2, 0:D]

        tok_loaded = [sem(f"tok_loaded{r}") for r in range(RING)]
        wr_loaded = sem("wr_loaded")
        weights_loaded = sem("weights_loaded")
        zeros_set = sem("zeros_set")
        zeros_stored = sem("zeros_stored")
        x1_stored = [sem(f"x1_stored{r}") for r in range(2)]
        row_stored = [sem(f"row_stored{r}") for r in range(RING)]
        const_step = sem("const_step")
        const_ready = sem("const_ready")
        stats1_ready, mv1_ready, ve1_ready, rstd1_ready, shift1_ready, xn_ready = map(sem, (
            "stats1_ready", "mv1_ready", "ve1_ready", "rstd1_ready", "shift1_ready", "xn_ready"))
        scores_ready, sbias_ready, probs_ready, srec_ready, vT_ready = map(sem, (
            "scores_ready", "sbias_ready", "probs_ready", "srec_ready", "vT_ready"))
        mix_ready, x1_ready = map(sem, ("mix_ready", "x1_ready"))
        stats2_ready, mv2_ready, ve2_ready, rstd2_ready, shift2_ready, row_ready = map(sem, (
            "stats2_ready", "mv2_ready", "ve2_ready", "rstd2_ready", "shift2_ready", "row_ready"))
        xnT_ready, xnT_copied, logits_ready, lbias_ready, lexp_ready = map(sem, (
            "xnT_ready", "xnT_copied", "logits_ready", "lbias_ready", "lexp_ready"))
        lrec_ready, p_ready, top_ready, topsum_ready, toprec_ready, marked_ready, chosen_ready = map(sem, (
            "lrec_ready", "p_ready", "top_ready", "topsum_ready", "toprec_ready", "marked_ready", "chosen_ready"))
        shares_ready, earlier_ready, rank_ready = map(sem, ("shares_ready", "earlier_ready", "rank_ready"))
        placed_ready, dest_ready, dest_split, dest_half_ready = map(sem, (
            "placed_ready", "dest_ready", "dest_split", "dest_half_ready"))
        slot_hot_ready, expert_hot_ready, expert_tok_ready, index_summed = map(sem, (
            "slot_hot_ready", "expert_hot_ready", "expert_tok_ready", "index_summed"))
        empty_ready, index_ready = map(sem, ("empty_ready", "index_ready"))
        gathered = [sem(f"gathered{r}") for r in range(RING)]
        scattered = [sem(f"scattered{n}") for n in range(SUMS)]
        xeT_ready, xeT_copied, gu_ready, sg_ready, h_ready = map(sem, (
            "xeT_ready", "xeT_copied", "gu_ready", "sg_ready", "h_ready"))
        hT_ready, hT_copied, ye_ready, ye_copied = map(sem, ("hT_ready", "hT_copied", "ye_ready", "ye_copied"))
        LAST = 4
        last_loaded = [sem(f"last_loaded{c}") for c in range(LAST)]
        last_added = sem("last_added")
        out_stored = sem("out_stored")

        block = ctx.enter_context(nc.Block())

        def run(eng, slots, total, step):
            def ok_at(s):
                return lambda lag: 0 <= s - lag < slots

            peel = 2 * UNROLL
            for s in range(peel):
                step(s, s % UNROLL, ok_at(s))
            with eng.Fori(peel, slots - UNROLL + 1, UNROLL) as base:
                for u in range(UNROLL):
                    step(base + u, u, lambda lag: True)
            for s in range(slots, total):
                step(s, s % UNROLL, ok_at(s))

        def reused(eng, semaphore, i, ring, per=1):
            if not isinstance(i, int) or i >= ring:
                eng.wait_ge(semaphore, per * (i - ring + 1))

        def wait_apart(eng, semaphore, value):
            if not isinstance(value, int):
                eng.compute_val(value)
                eng.wait_ge(const_ready, CONSTS)
            eng.wait_ge(semaphore, value)

        def dma_reused(eng, semaphores, i, r, ring):
            if not isinstance(i, int) or i >= ring:
                eng.wait_ge(semaphores[r], 16 * ((i - r) // ring) if isinstance(i, int)
                            else (i - r) * (16 // ring))

        @block.sync
        def _(sp):
            def load(t, r):
                sp.dma_start(tok_sb[:, r, :], tok[bass.ds(t * P, P), :]).then_inc(tok_loaded[r], 16)

            def keep(t, r):
                sp.wait_ge(x1_ready, t + 1)
                sp.dma_start(sums[0][bass.ds(t * P, P), :], x1[:, r % 2, :]).then_inc(x1_stored[r % 2], 16)

            def publish(t, r):
                sp.wait_ge(shares_ready, t + 1)
                sp.wait_ge(row_ready, t + 1)
                sp.dma_start(table[bass.ds(t * P, P), :], row[:, r, :]).then_inc(row_stored[r], 16)

            def weights(g):
                sp.dma_start(wgu_sb[:, bass.ds(g * GROUP, GROUP), :],
                             wgu[:, bass.ds(g * GROUP, GROUP), :]).then_inc(weights_loaded, 16)
                sp.dma_start(wd_sb[:, bass.ds(g * GROUP, GROUP), :],
                             wd[:, bass.ds(g * GROUP, GROUP), :]).then_inc(weights_loaded, 16)

            for t in range(RING):
                load(t, t)
            sp.dma_start(wr_sb[:, :, :], wr).then_inc(wr_loaded, 16)
            sp.wait_ge(zeros_set, 1)
            sp.dma_start(table[TOKENS:TOKENS + P, :], zeros).then_inc(zeros_stored, 16)
            sp.dma_start(sums[0][TOKENS:TOKENS + P, :], zeros[:, 0:D]).then_inc(zeros_stored, 16)
            for n in range(1, SUMS):
                sp.dma_start(sums[n].rearrange("(a p) d -> p a d", p=P),
                             zeros[:, 0:D].unsqueeze(1).broadcast_to([P, TOKENS // P + 1, D])
                             ).then_inc(zeros_stored, 16)

            def step(t, r, more):
                keep(t, r)
                if more:
                    load(t + RING, r)
                if not isinstance(t, int) or t >= 1:
                    publish(t - 1, (r - 1) % RING)

            for t in range(RING):
                step(t, t, True)
            sp.wait_ge(zeros_stored, 16 * (SUMS + 1))
            with sp.Fori(RING, TILES - RING - UNROLL + 1, UNROLL) as base:
                for u in range(UNROLL):
                    step(base + u, u, True)
                    weights(base + u - RING)
            for t in range(TILES - RING, TILES):
                step(t, t % RING, False)
            publish(TILES - 1, (TILES - 1) % RING)

            sp_last = [s.rearrange("(p a) d -> p (a d)", p=P) for s in (a[0:TOKENS, :] for a in sums)]
            out_view = out_rows.rearrange("(p a) d -> p (a d)", p=P)
            w = span // LAST
            for n in range(SUMS):
                sp.wait_ge(scattered[n], 16 * (EXPERTS // SUMS))
            for c in range(LAST):
                for n in range(SUMS):
                    sp.dma_start(last[n][:, c * w:(c + 1) * w], sp_last[n][:, c * w:(c + 1) * w]
                                 ).then_inc(last_loaded[c], 16)
            for c in range(LAST):
                sp.wait_ge(last_added, c + 1)
                sp.dma_start(out_view[:, c * w:(c + 1) * w], last[0][:, c * w:(c + 1) * w]).then_inc(out_stored, 16)
            sp.wait_ge(out_stored, 16 * LAST)

        @block.gpsimd
        def _(pool):
            def rstd(t, a, mv_ready, mv, ve_ready, ve, rstd_ready, out_, times):
                wait_apart(pool, mv_ready, t + 1)
                pool.tensor_scalar(ve[:, a:a + 1], mv[:, a, 1:2], EPS, times, ALU.add, ALU.mult).then_inc(ve_ready, 1)
                pool.wait_ge(ve_ready, t + 1)
                pool.tensor_tensor(out_[:, a:a + 1], ve[:, a:a + 1], neg_half[:, :], ALU.pow).then_inc(rstd_ready, 1)

            def rstd1_of(t, u):
                rstd(t, u % 2, mv1_ready, mv1, ve1_ready, ve1, rstd1_ready, rstd1, SCALE ** -2)

            def rstd2_of(t, u):
                rstd(t, u % 2, mv2_ready, mv2, ve2_ready, ve2, rstd2_ready, rstd2, 1.0)

            pool.memset(ident[:, :], 0.0).then_inc(const_step, 1)
            pool.memset(before[:, :], 1.0).then_inc(const_step, 1)
            pool.iota(pattern_i(0, CAP * TOPK), [[1, CAP], [0, TOPK]], base=0, channel_multiplier=0).then_inc(const_step, 1)
            pool.iota(pattern_i(1, EXPERTS * TOPK), [[1, EXPERTS], [0, TOPK]], base=1, channel_multiplier=0
                      ).then_inc(const_step, 1)
            pool.iota(pattern_i(2, EXPERTS), [[KEY // P, EXPERTS]], base=KEY // P, channel_multiplier=0
                      ).then_inc(const_step, 1)
            pool.iota(pattern_i(3, TILES), [[P, TILES]], base=1, channel_multiplier=1).then_inc(const_step, 1)
            pool.iota(pattern_i(4, 1), [[0, 1]], base=TOKENS + 1, channel_multiplier=1).then_inc(const_step, 1)
            pool.memset(neg_half[:, :], -0.5).then_inc(const_ready, 1)
            pool.memset(ones[:, :], 1.0).then_inc(const_ready, 1)
            pool.memset(earlier[:, 0, :], 0.0).then_inc(const_ready, 1)
            pool.wait_ge(const_step, 7)
            pool.affine_select(out=ident[:, :], in_=ident[:, :], compare_op=ALU.not_equal, fill=1.0, base=0,
                               pattern=[[-1, P]], channel_multiplier=1).then_inc(const_ready, 1)
            pool.affine_select(out=before[:, :], in_=before[:, :], compare_op=ALU.is_ge, fill=0.0, base=-1,
                               pattern=[[1, P]], channel_multiplier=-1).then_inc(const_ready, 1)
            pool.wait_ge(const_ready, 3)
            rstd1_of(0, 0)
            rstd1_of(1, 1)
            for n, to in enumerate((slot_no[:, :, :].rearrange("p a b -> p (a b)"),
                                    expert_no[:, :, :].rearrange("p a b -> p (a b)"),
                                    expert_key[:, :], token_no[:, :], spare[:, :])):
                pool.tensor_copy(to, pattern_i(n, to.shape[1])).then_inc(const_ready, 1)


            def step(s, u, ok):
                if ok(-2) and (not isinstance(s, int) or s >= 0):
                    rstd1_of(s + 2, u + 2)
                if ok(1):
                    rstd2_of(s - 1, u - 1)

            steps(pool, step)

            def gather(e):
                if e >= RING:
                    pool.wait_ge(h_ready, e - RING + 1)
                pool.indirect_dma_start(xe[:, e % RING, :], None, table,
                                        bass.IndirectOffsetOnAxis(ap=index[:, e:e + 1], axis=0)
                                        ).then_inc(gathered[e % RING], 16)

            def scatter(e):
                pool.wait_ge(ye_copied, e + 1)
                if e >= SUMS:
                    pool.wait_ge(scattered[e % SUMS], 16 * (e // SUMS))
                pool.indirect_dma_start(sums[e % SUMS], bass.IndirectOffsetOnAxis(ap=index[:, e:e + 1], axis=0),
                                        ye[:, e % RING, :], None, compute_op=ALU.add
                                        ).then_inc(scattered[e % SUMS], 16)

            pool.wait_ge(index_ready, 1)
            pool.wait_ge(zeros_stored, 16 * (SUMS + 1))
            for r in range(RING):
                pool.wait_ge(row_stored[r], 16 * (TILES // RING))
                pool.wait_ge(x1_stored[r % 2], 16 * (TILES // 2))
            gather(0)
            gather(1)
            for e in range(EXPERTS):
                if e + 2 < EXPERTS:
                    gather(e + 2)
                if e >= 3:
                    scatter(e - 3)
            for e in range(EXPERTS - 3, EXPERTS):
                scatter(e)
            for n in range(SUMS):
                pool.wait_ge(scattered[n], 16 * (EXPERTS // SUMS))

        @block.vector
        def _(dve):
            dve.memset(zeros, 0.0).then_inc(zeros_set, 1)

            def step(s, u, ok):
                n1, sm, n2, ro, sl = ok(-2), ok(0), ok(1), ok(2), ok(3)
                t0, a0, r0 = s + 2, (u + 2) % 2, (u + 2) % RING
                t1, a1, r1 = s, u % 2, u % RING
                t, a, r = s - 1, (u - 1) % 2, (u - 1) % RING
                t2, a2, r2 = s - 2, (u - 2) % 2, (u - 2) % RING
                t3, a3 = s - 3, (u - 3) % 2
                if sm:
                    dve.wait_ge(scores_ready, t1 + 1)
                    reused(dve, probs_ready, t1, 2, HALVES * DC)
                    dve.reduce_max(sbias[:, a1, :], scores_ps(a1).rearrange("p b (c d) -> p (b c) d", c=DC), axis=AX.X,
                                   negate=True).then_inc(sbias_ready, 1)
                if sl:
                    dve.wait_ge(rank_ready, t3 + 1)
                    dve.tensor_tensor(placed[:, a3, :], rank_ps(a3), chosen[:, a3, :], ALU.mult).then_inc(placed_ready, 1)
                if n1:
                    dve.wait_ge(tok_loaded[r0], 16 * (t0 // RING + 1) if isinstance(s, int)
                                else (t0 - r0) * (16 // RING) + 16)
                    reused(dve, xn_ready, t0, 2)
                    dve.bn_stats(stats1[:, a0, :], tok_sb[:, r0, 0:D]).then_inc(stats1_ready, 1)
                if sl:
                    wait_apart(dve, placed_ready, t3 + 1)
                    dve.max(dest[:, a3, :], placed[:, a3, :]).then_inc(dest_ready, 1)
                if n1:
                    wait_apart(dve, stats1_ready, t0 + 1)
                    dve.bn_aggr(mv1[:, a0, :], stats1[:, a0, :]).then_inc(mv1_ready, 1)
                if sl:
                    dve.wait_ge(dest_ready, t3 + 1)
                    dve.tensor_scalar(dest_parts[:, a3, 0, :], dest[:, a3, :], KEY - 1, None, ALU.bitwise_and
                                      ).then_inc(dest_split, 1)
                    dve.tensor_scalar(dest_parts[:, a3, 1, :], dest[:, a3, :], KEY_BITS, None,
                                      ALU.logical_shift_right).then_inc(dest_split, 1)
                if n2:
                    dve.wait_ge(mix_ready, t + 1)
                    dma_reused(dve, x1_stored, t, a, 2)
                    dve.tensor_tensor(x1[:, a, :], mix_ps, tok_sb[:, r, 0:D], ALU.add).then_inc(x1_ready, 1)
                if sl:
                    dve.wait_ge(dest_split, 2 * t3 + 2)
                    dve.tensor_copy(dest_half[:, a3, :, :], dest_parts[:, a3, :, :]).then_inc(dest_half_ready, 1)
                if n2:
                    dve.wait_ge(x1_ready, t + 1)
                    reused(dve, row_ready, t, 2)
                    dve.bn_stats(stats2[:, a, :], x1[:, a, :]).then_inc(stats2_ready, 1)
                if sl:
                    dve.wait_ge(dest_half_ready, t3 + 1)
                    if not isinstance(s, int) or t3 >= 1:
                        dve.wait_ge(expert_tok_ready, t3)
                    dve.tensor_tensor(expert_hot[:, :, :], expert_no[:, :, :],
                                      dest_half[:, a3, 1, :].unsqueeze(1).broadcast_to([P, EXPERTS, TOPK]), ALU.is_equal
                                      ).then_inc(expert_hot_ready, 1)
                if n2:
                    wait_apart(dve, stats2_ready, t + 1)
                    dve.bn_aggr(mv2[:, a, :], stats2[:, a, :]).then_inc(mv2_ready, 1)
                if ro:
                    dve.wait_ge(logits_ready, t2 + 1)
                    dve.reduce_max(lbias[:, a2:a2 + 1], logits_ps(a2), axis=AX.X, negate=True).then_inc(lbias_ready, 1)
                if sl:
                    reused(dve, index_summed, t3, 2)
                    dve.tensor_tensor(slot_hot[:, a3, :, :], slot_no[:, :, :],
                                      dest_half[:, a3, 0, :].unsqueeze(1).broadcast_to([P, CAP, TOPK]), ALU.is_equal
                                      ).then_inc(slot_hot_ready, 1)
                if n1:
                    dve.wait_ge(rstd1_ready, t0 + 1)
                    dve.scalar_tensor_tensor(shift1[:, a0:a0 + 1], mv1[:, a0, 0:1], -1.0, rstd1[:, a0:a0 + 1],
                                             ALU.mult, ALU.mult).then_inc(shift1_ready, 1)
                if n2:
                    dve.wait_ge(rstd2_ready, t + 1)
                    dve.scalar_tensor_tensor(shift2[:, a:a + 1], mv2[:, a, 0:1], -1.0, rstd2[:, a:a + 1],
                                             ALU.mult, ALU.mult).then_inc(shift2_ready, 1)
                if sm:
                    dve.wait_ge(probs_ready, HALVES * DC * (t1 + 1))
                    dve.reciprocal(srec[:, a1, :], ssum[:, a1, :]).then_inc(srec_ready, 1)
                if ro:
                    dve.wait_ge(lexp_ready, t2 + 1)
                    dve.reciprocal(lrec[:, a2:a2 + 1], lsum[:, a2:a2 + 1]).then_inc(lrec_ready, 1)
                if sm:
                    dve.wait_ge(srec_ready, t1 + 1)
                    reused(dve, mix_ready, t1, 2)
                    dve.tensor_tensor(vT[:, a1, :].rearrange("p (n s) -> p n s", s=SEQ),
                                      tok_sb[:, r1, 2 * D:3 * D].rearrange("p (n s) -> p n s", s=SEQ),
                                      srec[:, a1, :].unsqueeze(2).broadcast_to([P, HALVES * DC, SEQ]), ALU.mult
                                      ).then_inc(vT_ready, 1)
                if ro:
                    dve.wait_ge(lrec_ready, t2 + 1)
                    dve.tensor_scalar(p_all[:, a2, :], lexp[:, a2, :], lrec[:, a2:a2 + 1], None, ALU.mult
                                      ).then_inc(p_ready, 1)
                    wait_apart(dve, p_ready, t2 + 1)
                    dve.max(p_top[:, a2, :], p_all[:, a2, :]).then_inc(top_ready, 1)
                    wait_apart(dve, top_ready, t2 + 1)
                    dve.match_replace(p_marked[:, a2, :], p_top[:, a2, :], p_all[:, a2, :], -1.0
                                      ).then_inc(marked_ready, 1)
                    dve.reduce_sum(p_topsum[:, a2:a2 + 1], p_top[:, a2, :], axis=AX.X).then_inc(topsum_ready, 1)
                    dve.wait_ge(marked_ready, t2 + 1)
                    dve.tensor_scalar(chosen[:, a2, :], p_marked[:, a2, :], 0.0, None, ALU.is_lt
                                      ).then_inc(chosen_ready, 1)
                    dve.wait_ge(topsum_ready, t2 + 1)
                    dve.reciprocal(p_toprec[:, a2:a2 + 1], p_topsum[:, a2:a2 + 1]).then_inc(toprec_ready, 1)
                    dve.wait_ge(chosen_ready, t2 + 1)
                    if not isinstance(s, int) or t2 >= 1:
                        dve.wait_ge(earlier_ready, t2)
                    reused(dve, rank_ready, t2, RING - 1)
                    dve.tensor_tensor(earlier[:, (r2 + 1) % RING, :], earlier[:, r2, :], chosen[:, a2, :], ALU.add
                                      ).then_inc(earlier_ready, 1)
                    dve.wait_ge(toprec_ready, t2 + 1)
                    dve.scalar_tensor_tensor(row[:, r2, D:ROW], p_all[:, a2, :], p_toprec[:, a2:a2 + 1],
                                             chosen[:, a2, :], ALU.mult, ALU.mult).then_inc(shares_ready, 1)

            steps(dve, step, lambda: dve.wait_ge(const_ready, CONSTS))

            dve.wait_ge(index_summed, TILES)
            dve.tensor_scalar(empty, index_ps, 0.0, spare[:, 0:1], ALU.is_equal, ALU.mult).then_inc(empty_ready, 1)
            dve.wait_ge(empty_ready, 1)
            dve.scalar_tensor_tensor(index[:, :], index_ps, -1.0, empty, ALU.add, ALU.add
                                     ).then_inc(index_ready, 1)

            def step_e(s, u, ok):
                if ok(1):
                    e, a, r = s - 1, (u - 1) % 2, (u - 1) % RING
                    dve.wait_ge(sg_ready, e + 1)
                    reused(dve, hT_ready, e, 2)
                    dve.scalar_tensor_tensor(h[:, a, :], gu_ps(a)[:, INNER:2 * INNER],
                                             xe[:, r, bass.ds(e + D, 1)], sg[:, a, :], ALU.mult, ALU.mult
                                             ).then_inc(h_ready, 1)
                if ok(2):
                    e, a = s - 2, (u - 2) % 2
                    dve.wait_ge(hT_ready, e + 1)
                    reused(dve, ye_ready, e, 2)
                    dve.tensor_copy(hT[:, a, :], hT_ps(a)).then_inc(hT_copied, 1)

            run(dve, EXPERTS, EXPERTS + 3, step_e)

            w = span // LAST
            for c in range(LAST):
                dve.wait_ge(last_loaded[c], 16 * SUMS)
                dve.tensor_tensor(last[0][:, c * w:(c + 1) * w], last[0][:, c * w:(c + 1) * w],
                                  last[1][:, c * w:(c + 1) * w], ALU.add).then_inc(last_added, 1)

        @block.scalar
        def _(act):
            def step(s, u, ok):
                if ok(2):
                    t, a = s - 2, (u - 2) % 2
                    act.wait_ge(xnT_ready, t + 1)
                    reused(act, logits_ready, t, 2)
                    act.activation(xnT[:, a, :], xnT_ps(a), ACT.Copy).then_inc(xnT_copied, 1)
                if ok(0):
                    t, a = s, u % 2
                    act.wait_ge(sbias_ready, t + 1)
                    reused(act, mix_ready, t, 2)
                    reused(act, srec_ready, t, 2)
                    for n in range(HALVES * DC):
                        act.activation(probs[:, a, n * D:(n + 1) * D],
                                       scores_ps(a)[:, n // DC, (n % DC) * D:(n % DC + 1) * D],
                                       ACT.Exp, bias=sbias[:, a, n:n + 1], accum_out=ssum[:, a, n:n + 1]
                                       ).then_inc(probs_ready, 1)
                if ok(3):
                    t = s - 3
                    act.wait_ge(expert_hot_ready, t + 1)
                    if not isinstance(s, int) or t >= 1:
                        act.wait_ge(index_summed, t)
                    act.activation(expert_tok[:, :, :], expert_hot[:, :, :], ACT.Copy, scale=token_no[:, bass.ds(t, 1)]
                                   ).then_inc(expert_tok_ready, 1)
                if ok(2):
                    t, a = s - 2, (u - 2) % 2
                    act.wait_ge(lbias_ready, t + 1)
                    reused(act, p_ready, t, 2)
                    act.activation(lexp[:, a, :], logits_ps(a), ACT.Exp, bias=lbias[:, a:a + 1],
                                   accum_out=lsum[:, a:a + 1]).then_inc(lexp_ready, 1)
                if ok(-2):
                    t, a, r = s + 2, (u + 2) % 2, (u + 2) % RING
                    act.wait_ge(shift1_ready, t + 1)
                    reused(act, scores_ready, t, 2)
                    act.activation(xn[:, a, :], tok_sb[:, r, 0:D], ACT.Identity, scale=rstd1[:, a:a + 1],
                                   bias=shift1[:, a:a + 1]).then_inc(xn_ready, 1)
                if ok(1):
                    t, a, r = s - 1, (u - 1) % 2, (u - 1) % RING
                    act.wait_ge(shift2_ready, t + 1)
                    dma_reused(act, row_stored, t, r, RING)
                    act.activation(row[:, r, 0:D], x1[:, a, :], ACT.Identity, scale=rstd2[:, a:a + 1],
                                   bias=shift2[:, a:a + 1]).then_inc(row_ready, 1)

            steps(act, step, lambda: act.wait_ge(const_ready, CONSTS))

            def step_e(s, u, ok):
                if ok(0):
                    e, a = s, u % 2
                    act.wait_ge(xeT_ready, e + 1)
                    reused(act, gu_ready, e, 2)
                    act.activation(xeT[:, a, :], xeT_ps(a), ACT.Copy).then_inc(xeT_copied, 1)
                if ok(1):
                    e, a = s - 1, (u - 1) % 2
                    act.wait_ge(gu_ready, e + 1)
                    reused(act, h_ready, e, 2)
                    act.activation(sg[:, a, :], gu_ps(a)[:, 0:INNER], ACT.Silu).then_inc(sg_ready, 1)
                if ok(3):
                    e, a, r = s - 3, (u - 3) % 2, (u - 3) % RING
                    act.wait_ge(ye_ready, e + 1)
                    if not isinstance(e, int) or e >= RING:
                        act.wait_ge(scattered[a], ((e - RING) // SUMS + 1) * 16 if isinstance(e, int)
                                    else (e - RING - a) * (16 // SUMS) + 16)
                    act.activation(ye[:, r, :], ye_ps(a), ACT.Copy).then_inc(ye_copied, 1)

            run(act, EXPERTS, EXPERTS + 3, step_e)

        @block.tensor
        def _(pe):
            pe.wait_ge(const_ready, CONSTS)
            pe.wait_ge(wr_loaded, 16)

            def scores(t, u):
                a, r = u % 2, u % RING
                pe.wait_ge(xn_ready, t + 1)
                reused(pe, probs_ready, t, 2, HALVES * DC)
                for c in range(DC):
                    for b in range(HALVES):
                        rows = slice(b * SEQ, (b + 1) * SEQ)
                        mm = pe.matmul(scores_ps(a)[:, b, c * D:(c + 1) * D],
                                       tok_sb[rows, r, D + c * P:D + (c + 1) * P], xn[rows, a, :], start=True, stop=True)
                mm.then_inc(scores_ready, 1)

            def mix(t, u):
                a = u % 2
                pe.wait_ge(vT_ready, t + 1)
                if not isinstance(t, int) or t >= 1:
                    pe.wait_ge(x1_ready, t)
                for c in range(DC):
                    for b in range(HALVES):
                        n = b * DC + c
                        mm = pe.matmul(mix_ps[b * SEQ:(b + 1) * SEQ, :], vT[:, a, n * SEQ:(n + 1) * SEQ],
                                       probs[:, a, n * D:(n + 1) * D], start=(c == 0), stop=(c == DC - 1))
                mm.then_inc(mix_ready, 1)

            def turn(t, u):
                a, r = u % 2, u % RING
                pe.wait_ge(row_ready, t + 1)
                reused(pe, placed_ready, t, 2)
                for c in range(DC):
                    mm = pe.transpose(xnT_ps(a)[:, c * P:(c + 1) * P], row[:, r, c * P:(c + 1) * P], ident[:, :])
                mm.then_inc(xnT_ready, 1)

            def logits(t, u):
                a = u % 2
                pe.wait_ge(xnT_copied, t + 1)
                for c in range(DC):
                    mm = pe.matmul(logits_ps(a), xnT[:, a, c * P:(c + 1) * P], wr_sb[:, c, :],
                                   start=(c == 0), stop=(c == DC - 1))
                mm.then_inc(logits_ready, 1)

            def rank(t, u):
                a, r = u % 2, u % RING
                pe.wait_ge(chosen_ready, t + 1)
                if not isinstance(t, int) or t >= 1:
                    pe.wait_ge(earlier_ready, t)
                pe.matmul(rank_ps(a), ones[:, :], expert_key[:, :], start=True, stop=False)
                pe.matmul(rank_ps(a), before[:, :], chosen[:, a, :], start=False, stop=False)
                pe.matmul(rank_ps(a), ones[:, :], earlier[:, r, :], start=False, stop=True).then_inc(rank_ready, 1)

            def index_add(t, u):
                a = u % 2
                pe.wait_ge(slot_hot_ready, t + 1)
                pe.wait_ge(expert_tok_ready, t + 1)
                first = isinstance(t, int) and t == 0
                for k in range(TOPK):
                    mm = pe.matmul(index_ps, slot_hot[:, a, :, k], expert_tok[:, :, k],
                                   start=(first and k == 0),
                                   stop=(isinstance(t, int) and t == TILES - 1 and k == TOPK - 1))
                mm.then_inc(index_summed, 1)

            def step(s, u, ok):
                if ok(3):
                    rank(s - 3, u - 3)
                if ok(2):
                    turn(s - 2, u - 2)
                if ok(1):
                    mix(s - 1, u - 1)
                if ok(2):
                    logits(s - 2, u - 2)
                if ok(-1):
                    scores(s + 1, u + 1)
                if ok(3):
                    index_add(s - 3, u - 3)

            steps(pe, step)

            pe.wait_ge(weights_loaded, 16 * 2 * GROUPS)

            def step_e(s, u, ok):
                if ok(0):
                    e, a, r = s, u % 2, u % RING
                    pe.wait_ge(gathered[r], 16 * (e // RING + 1) if isinstance(e, int) else (e - r) * (16 // RING) + 16)
                    reused(pe, xeT_copied, e, 2)
                    for c in range(DC):
                        mm = pe.transpose(xeT_ps(a)[:, c * P:(c + 1) * P], xe[:, r, c * P:(c + 1) * P], ident[:, :])
                    mm.then_inc(xeT_ready, 1)
                if ok(2):
                    e, a = s - 2, (u - 2) % 2
                    pe.wait_ge(h_ready, e + 1)
                    reused(pe, hT_copied, e, 2)
                    pe.transpose(hT_ps(a), h[:, a, :], ident[:, :]).then_inc(hT_ready, 1)
                if ok(1):
                    e, a = s - 1, (u - 1) % 2
                    pe.wait_ge(xeT_copied, e + 1)
                    reused(pe, h_ready, e, 2)
                    for c in range(DC):
                        mm = pe.matmul(gu_ps(a), xeT[:, a, c * P:(c + 1) * P],
                                       wgu_sb[:, bass.ds(e, 1), c * 2 * INNER:(c + 1) * 2 * INNER],
                                       start=(c == 0), stop=(c == DC - 1))
                    mm.then_inc(gu_ready, 1)
                if ok(3):
                    e, a = s - 3, (u - 3) % 2
                    pe.wait_ge(hT_copied, e + 1)
                    reused(pe, ye_copied, e, 2)
                    pe.matmul(ye_ps(a), hT[:, a, :], wd_sb[:, bass.ds(e, 1), :], start=True, stop=True
                              ).then_inc(ye_ready, 1)

            run(pe, EXPERTS, EXPERTS + 3, step_e)


CONSTS = 10
KEY_BITS = KEY.bit_length() - 1
SCALE = float(D) ** -0.5


def steps(eng, step, before_items=lambda: None):
    first = UNROLL + 1
    last = TILES - 3

    def ok_at(s):
        return lambda lag: 0 <= s - lag < TILES

    for s in range(-2, first):
        if s == 0:
            before_items()
        step(s, s, ok_at(s))
    with eng.Fori(first, last - UNROLL + 1, UNROLL) as base:
        for u in range(UNROLL):
            step(base + u, first + u, lambda lag: True)
    for s in range(last, TILES + 3):
        step(s, s, ok_at(s))


def kernel(**inputs):
    import concourse.bacc as _bacc
    from concourse.bass_utils import run_bass_kernel_spmd as _run

    x = np.asarray(inputs["x"]).reshape(TOKENS, D)
    c = np.asarray(inputs["ctx_2048"])
    cT = c.reshape(TILES, HALVES, SEQ, DC, P).transpose(0, 4, 1, 3, 2).reshape(TOKENS, D)
    gate, up = (np.asarray(inputs[n]).reshape(EXPERTS, DC, P, INNER) for n in ("L0_ffn_gate_proj", "L0_ffn_up_proj"))
    arrays = {
        "tok": np.concatenate([x, c.reshape(TOKENS, D), cT], axis=1),
        "wgu": np.stack([gate, up], axis=3).transpose(2, 0, 1, 3, 4).reshape(P, EXPERTS, DC * 2 * INNER),
        "wd": np.asarray(inputs["L0_ffn_down_proj"]).transpose(1, 0, 2),
        "wr": np.asarray(inputs["L0_ffn_router_weight"]).reshape(DC, P, EXPERTS).transpose(1, 0, 2),
    }
    arrays = {k: np.ascontiguousarray(v) for k, v in arrays.items()}
    nc = _bacc.Bacc("TRN2", target_bir_lowering=False, num_devices=1)
    args = [nc.dram_tensor(f"in_{k}", v.shape, F32, kind="ExternalInput").ap() for k, v in arrays.items()]
    out = nc.dram_tensor("out_x", (BATCH, SEQ, D), F32, kind="ExternalOutput").ap()
    build(nc, *args, out)
    r = _run(nc, [{f"in_{k}": v for k, v in arrays.items()}], core_ids=[0])
    return r.results[0]["out_x"]
```

```python
from contextlib import ExitStack

import numpy as np

import concourse.bass as bass
from concourse import mybir

P = 128
BATCH, SEQ, D = 32, 64, 256
TOKENS = BATCH * SEQ
TILES = TOKENS // P
HALVES = P // SEQ
DC = D // P
EXPERTS, INNER, TOPK = 64, 96, 8
CAP = 2 * (512 * TOPK) // EXPERTS
ROW = D + EXPERTS
UNROLL = 4
RING = 4
XRING = 8
LEAD = 7
SUMS = 2
GROUP = 4
GROUPS = EXPERTS // GROUP
AHEAD = 2
EPS = 1e-5
KEY = TOKENS

F32 = mybir.dt.float32
F16 = mybir.dt.float16
I32 = mybir.dt.int32
U32 = mybir.dt.uint32
ALU = mybir.AluOpType
ACT = mybir.ActivationFunctionType
AX = mybir.AxisListType


def build(nc, tok, wgu, wd, wr, out):
    table = nc.dram_tensor("table", [TOKENS + P, ROW], F32, kind="Internal").ap()
    sums = [nc.dram_tensor(f"sum{n}", [TOKENS + P, D], F32, kind="Internal").ap() for n in range(SUMS)]
    out_rows = out.rearrange("b s d -> (b s) d")

    with ExitStack() as ctx:
        def sb(name, shape, dt=F32):
            return ctx.enter_context(nc.sbuf_tensor(name, shape, dt))

        def sem(name):
            return ctx.enter_context(nc.semaphore(name))

        wgu_sb = sb("wgu_sb", [P, EXPERTS, DC * 2 * INNER])
        wd_sb = sb("wd_sb", [INNER, EXPERTS, D])
        wr_sb = sb("wr_sb", [P, DC, EXPERTS])
        tok_sb = sb("tok_sb", [P, RING, 3 * D])
        xn = sb("xn", [P, 2, D])
        probs = sb("probs", [P, 2, HALVES * DC * D])
        vT = sb("vT", [P, 2, HALVES * DC * SEQ])
        x1 = sb("x1", [P, 2, D])
        row = sb("row", [P, RING, ROW])
        xnT = sb("xnT", [P, 2, D])
        slot_hot = sb("slot_hot", [P, 2, CAP, TOPK], F16)
        expert_hot = sb("expert_hot", [P, EXPERTS, TOPK], F16)
        expert_tok = sb("expert_tok", [P, EXPERTS, TOPK], F16)
        ident = sb("ident", [P, P])
        before = sb("before", [P, P], F16)
        ones = sb("ones", [P, P], F16)
        slot_no = sb("slot_no", [P, CAP, TOPK], F16)
        expert_no = sb("expert_no", [P, EXPERTS, TOPK], F16)
        expert_key = sb("expert_key", [P, EXPERTS], F16)
        token_no = sb("token_no", [P, TILES])
        spare = sb("spare", [P, 1])
        neg_half = sb("neg_half", [P, 1])
        stats1 = sb("stats1", [P, 2, 6])
        stats2 = sb("stats2", [P, 2, 6])
        mv1 = sb("mv1", [P, 2, 2])
        mv2 = sb("mv2", [P, 2, 2])
        ve1 = sb("ve1", [P, 2])
        ve2 = sb("ve2", [P, 2])
        rstd1 = sb("rstd1", [P, 2])
        rstd2 = sb("rstd2", [P, 2])
        sbias = sb("sbias", [P, 2, HALVES * DC])
        ssum = sb("ssum", [P, 2, HALVES * DC])
        srec = sb("srec", [P, 2, HALVES * DC])
        lbias = sb("lbias", [P, 2])
        lexp = sb("lexp", [P, 2, EXPERTS])
        lsum = sb("lsum", [P, 2])
        lrec = sb("lrec", [P, 2])
        p_all = sb("p_all", [P, 2, EXPERTS])
        p_top = sb("p_top", [P, 2, TOPK])
        p_topsum = sb("p_topsum", [P, 2])
        p_toprec = sb("p_toprec", [P, 2])
        p_marked = sb("p_marked", [P, 2, EXPERTS])
        chosen = sb("chosen", [P, 2, EXPERTS], F16)
        earlier = sb("earlier", [P, RING, EXPERTS], F16)
        placed = sb("placed", [P, 2, EXPERTS])
        dest = sb("dest", [P, 2, TOPK], I32)
        dest_parts = sb("dest_parts", [P, 2, 2, TOPK], I32)
        dest_half = sb("dest_half", [P, 2, 2, TOPK], F16)
        shift1 = sb("shift1", [P, 2])
        shift2 = sb("shift2", [P, 2])
        index = sb("index", [P, EXPERTS], U32)

        flat_probs = probs[:, :, :].rearrange("p a f -> p (a f)")
        xe = [flat_probs[:, r * ROW:(r + 1) * ROW] for r in range(RING)] + [row[:, r, :] for r in range(RING)]
        xeT = flat_probs[:, RING * ROW:RING * ROW + 2 * D].rearrange("p (a f) -> p a f", a=2)
        flat_tok = tok_sb[:, :, :].rearrange("p a f -> p (a f)")
        at = RING * D
        empty = placed[:, 0, :]
        ye = flat_tok[:, 0:at].rearrange("p (r f) -> p r f", r=RING)
        sg = flat_tok[:, at:at + 2 * INNER].rearrange("p (a f) -> p a f", a=2)
        at += 2 * INNER
        h = flat_tok[:, at:at + 2 * INNER].rearrange("p (a f) -> p a f", a=2)
        at += 2 * INNER
        hT = flat_tok[0:INNER, at:at + 2 * P].rearrange("p (a f) -> p a f", a=2)
        zeros = wgu_sb[:, EXPERTS - 1, 0:ROW]
        pattern_of = [slot_no[:, :, :].rearrange("p a b -> p (a b)"), expert_no[:, :, :].rearrange("p a b -> p (a b)"),
                      expert_key[:, :], token_no[:, :], spare[:, :]]
        first = EXPERTS - 1 - 3 * len(pattern_of)
        patterns = [wgu_sb[:, first + 3 * n:first + 3 * n + 3, :].rearrange("p e f -> p (e f)")[:, 0:to.shape[1]].bitcast(I32)
                    for n, to in enumerate(pattern_of)]

        flat_w = wgu_sb[:, :, :].rearrange("p e f -> p (e f)")
        span = TOKENS // P * D
        last = [flat_w[:, n * span:(n + 1) * span] for n in range(SUMS)]

        ps = ctx.enter_context(nc.psum_tensor("ps", [P, 8, 512], F32))

        def scores_ps(t2):
            return ps[:, 2 * t2:2 * t2 + 2, :]

        mix_ps = ps[:, 4, 0:D]
        index_ps = ps[:, 5, 0:EXPERTS]

        def xnT_ps(t2):
            return ps[:, 6 + t2, 0:D]

        def logits_ps(t2):
            return ps[:, 6 + t2, D:D + EXPERTS]

        def rank_ps(t2):
            return ps[:, 6 + t2, D + EXPERTS:D + 2 * EXPERTS]

        def xeT_ps(e2):
            return ps[:, e2, 0:D]

        def gu_ps(e2):
            return ps[:, 2 + e2, 0:2 * INNER]

        def hT_ps(e2):
            return ps[0:INNER, 4 + e2, 0:P]

        def ye_ps(e2):
            return ps[:, 6 + e2, 0:D]

        tok_loaded = [sem(f"tok_loaded{r}") for r in range(RING)]
        wr_loaded = sem("wr_loaded")
        weights_loaded = sem("weights_loaded")
        zeros_set = sem("zeros_set")
        zeros_stored = sem("zeros_stored")
        x1_stored = [sem(f"x1_stored{r}") for r in range(2)]
        row_stored = [sem(f"row_stored{r}") for r in range(RING)]
        const_step = sem("const_step")
        pattern_ready = sem("pattern_ready")
        const_ready = sem("const_ready")
        stats1_ready, mv1_ready, ve1_ready, rstd1_ready, shift1_ready, xn_ready = map(sem, (
            "stats1_ready", "mv1_ready", "ve1_ready", "rstd1_ready", "shift1_ready", "xn_ready"))
        scores_ready, sbias_ready, probs_ready, srec_ready, vT_ready = map(sem, (
            "scores_ready", "sbias_ready", "probs_ready", "srec_ready", "vT_ready"))
        mix_ready, x1_ready = map(sem, ("mix_ready", "x1_ready"))
        stats2_ready, mv2_ready, ve2_ready, rstd2_ready, shift2_ready, row_ready = map(sem, (
            "stats2_ready", "mv2_ready", "ve2_ready", "rstd2_ready", "shift2_ready", "row_ready"))
        xnT_ready, xnT_copied, logits_ready, lbias_ready, lexp_ready = map(sem, (
            "xnT_ready", "xnT_copied", "logits_ready", "lbias_ready", "lexp_ready"))
        lrec_ready, p_ready, top_ready, topsum_ready, toprec_ready, marked_ready, chosen_ready = map(sem, (
            "lrec_ready", "p_ready", "top_ready", "topsum_ready", "toprec_ready", "marked_ready", "chosen_ready"))
        shares_ready, earlier_ready, rank_ready = map(sem, ("shares_ready", "earlier_ready", "rank_ready"))
        placed_ready, dest_ready, dest_split, dest_half_ready = map(sem, (
            "placed_ready", "dest_ready", "dest_split", "dest_half_ready"))
        slot_hot_ready, expert_hot_ready, expert_tok_ready, index_summed = map(sem, (
            "slot_hot_ready", "expert_hot_ready", "expert_tok_ready", "index_summed"))
        empty_ready, index_ready = map(sem, ("empty_ready", "index_ready"))
        gathered = [sem(f"gathered{r}") for r in range(XRING)]
        scattered = [sem(f"scattered{n}") for n in range(SUMS)]
        xeT_ready, xeT_copied, gu_ready, sg_ready, h_ready = map(sem, (
            "xeT_ready", "xeT_copied", "gu_ready", "sg_ready", "h_ready"))
        hT_ready, hT_copied, ye_ready, ye_copied = map(sem, ("hT_ready", "hT_copied", "ye_ready", "ye_copied"))
        LAST = 8
        last_loaded = [sem(f"last_loaded{c}") for c in range(LAST)]
        last_added = sem("last_added")
        out_stored = sem("out_stored")

        block = ctx.enter_context(nc.Block())

        def run(eng, step):
            def ok_at(s):
                return lambda lag: 0 <= s - lag < EXPERTS

            for s in range(XRING):
                step(s, s, ok_at(s))
            with eng.Fori(XRING, EXPERTS - XRING + 1, XRING) as base:
                for u in range(XRING):
                    step(base + u, u, lambda lag: True)
            for s in range(EXPERTS, EXPERTS + 3):
                step(s, s % XRING, ok_at(s))

        def reused(eng, semaphore, i, ring, per=1):
            if not isinstance(i, int) or i >= ring:
                eng.wait_ge(semaphore, per * (i - ring + 1))

        def wait_apart(eng, semaphore, value):
            if not isinstance(value, int):
                eng.compute_val(value)
                eng.wait_ge(const_ready, CONSTS)
            eng.wait_ge(semaphore, value)

        def dma_reused(eng, semaphores, i, r, ring):
            if not isinstance(i, int) or i >= ring:
                eng.wait_ge(semaphores[r], 16 * ((i - r) // ring) if isinstance(i, int)
                            else (i - r) * (16 // ring))

        @block.sync
        def _(sp):
            def load(t, r):
                sp.dma_start(tok_sb[:, r, :], tok[bass.ds(t * P, P), :]).then_inc(tok_loaded[r], 16)

            def keep(t, r):
                sp.wait_ge(x1_ready, t + 1)
                sp.dma_start(sums[0][bass.ds(t * P, P), :], x1[:, r % 2, :]).then_inc(x1_stored[r % 2], 16)

            def publish(t, r):
                sp.wait_ge(shares_ready, t + 1)
                sp.wait_ge(row_ready, t + 1)
                sp.dma_start(table[bass.ds(t * P, P), :], row[:, r, :]).then_inc(row_stored[r], 16)

            def weights(g):
                sp.dma_start(wgu_sb[:, bass.ds(g * GROUP, GROUP), :],
                             wgu[:, bass.ds(g * GROUP, GROUP), :]).then_inc(weights_loaded, 16)
                sp.dma_start(wd_sb[:, bass.ds(g * GROUP, GROUP), :],
                             wd[:, bass.ds(g * GROUP, GROUP), :]).then_inc(weights_loaded, 16)

            for t in range(RING):
                load(t, t)
            sp.dma_start(wr_sb[:, :, :], wr).then_inc(wr_loaded, 16)
            sp.wait_ge(zeros_set, 1)
            sp.dma_start(table[TOKENS:TOKENS + P, :], zeros).then_inc(zeros_stored, 16)
            sp.dma_start(sums[0][TOKENS:TOKENS + P, :], zeros[:, 0:D]).then_inc(zeros_stored, 16)
            for n in range(1, SUMS):
                sp.dma_start(sums[n].rearrange("(a p) d -> p a d", p=P),
                             zeros[:, 0:D].unsqueeze(1).broadcast_to([P, TOKENS // P + 1, D])
                             ).then_inc(zeros_stored, 16)

            for g in range(AHEAD):
                weights(g)

            def step(t, r, more):
                keep(t, r)
                if more:
                    load(t + RING, r)
                if not isinstance(t, int) or t >= 1:
                    publish(t - 1, (r - 1) % RING)

            for t in range(RING):
                step(t, t, True)
                weights(t + AHEAD)
            sp.wait_ge(zeros_stored, 16 * (SUMS + 1))
            with sp.Fori(RING, TILES - RING - UNROLL + 1, UNROLL) as base:
                for u in range(UNROLL):
                    step(base + u, u, True)
                    weights(base + u + AHEAD)
            for t in range(TILES - RING, TILES):
                step(t, t % RING, False)
                if t + AHEAD < GROUPS:
                    weights(t + AHEAD)
            publish(TILES - 1, (TILES - 1) % RING)

            sp_last = [s.rearrange("(p a) d -> p (a d)", p=P) for s in (a[0:TOKENS, :] for a in sums)]
            out_view = out_rows.rearrange("(p a) d -> p (a d)", p=P)
            w = span // LAST
            for n in reversed(range(SUMS)):
                sp.wait_ge(scattered[n], 16 * SCATTERS[n])
                for c in range(LAST):
                    sp.dma_start(last[n][:, c * w:(c + 1) * w], sp_last[n][:, c * w:(c + 1) * w]
                                 ).then_inc(last_loaded[c], 16)
            for c in range(LAST):
                sp.wait_ge(last_added, c + 1)
                sp.dma_start(out_view[:, c * w:(c + 1) * w], last[0][:, c * w:(c + 1) * w]).then_inc(out_stored, 16)
            sp.wait_ge(out_stored, 16 * LAST)

        @block.gpsimd
        def _(pool):
            def rstd(t, a, mv_ready, mv, ve_ready, ve, rstd_ready, out_, shift_ready, shift, times):
                wait_apart(pool, mv_ready, t + 1)
                pool.tensor_scalar(ve[:, a:a + 1], mv[:, a, 1:2], EPS, times, ALU.add, ALU.mult).then_inc(ve_ready, 1)
                pool.wait_ge(ve_ready, t + 1)
                pool.tensor_tensor(out_[:, a:a + 1], ve[:, a:a + 1], neg_half[:, :], ALU.pow).then_inc(rstd_ready, 1)
                wait_apart(pool, rstd_ready, t + 1)
                pool.tensor_scalar(shift[:, a:a + 1], mv[:, a, 0:1], out_[:, a:a + 1], -1.0, ALU.mult, ALU.mult
                                   ).then_inc(shift_ready, 1)

            def rstd1_of(t, u):
                rstd(t, u % 2, mv1_ready, mv1, ve1_ready, ve1, rstd1_ready, rstd1, shift1_ready, shift1, SCALE ** -2)

            def rstd2_of(t, u):
                rstd(t, u % 2, mv2_ready, mv2, ve2_ready, ve2, rstd2_ready, rstd2, shift2_ready, shift2, 1.0)

            pool.memset(neg_half[:, :], -0.5).then_inc(const_ready, 1)
            pool.memset(ident[:, :], 0.0).then_inc(const_step, 1)
            pool.memset(before[:, :], 1.0).then_inc(const_step, 1)
            pool.iota(patterns[0], [[1, CAP], [0, TOPK]], base=0, channel_multiplier=0).then_inc(pattern_ready, 1)
            pool.iota(patterns[1], [[1, EXPERTS], [0, TOPK]], base=1, channel_multiplier=0
                      ).then_inc(pattern_ready, 1)
            pool.wait_ge(const_ready, 1)
            rstd1_of(0, 0)
            rstd1_of(1, 1)
            pool.iota(patterns[2], [[KEY // P, EXPERTS]], base=KEY // P, channel_multiplier=0
                      ).then_inc(pattern_ready, 1)
            pool.iota(patterns[3], [[P, TILES]], base=1, channel_multiplier=1).then_inc(pattern_ready, 1)
            pool.iota(patterns[4], [[0, 1]], base=TOKENS + 1, channel_multiplier=1).then_inc(pattern_ready, 1)
            pool.memset(ones[:, :], 1.0).then_inc(const_ready, 1)
            pool.memset(earlier[:, 0, :], 0.0).then_inc(const_ready, 1)
            pool.wait_ge(const_step, 2)
            pool.affine_select(out=ident[:, :], in_=ident[:, :], compare_op=ALU.not_equal, fill=1.0, base=0,
                               pattern=[[-1, P]], channel_multiplier=1).then_inc(const_ready, 1)
            pool.affine_select(out=before[:, :], in_=before[:, :], compare_op=ALU.is_ge, fill=0.0, base=-1,
                               pattern=[[1, P]], channel_multiplier=-1).then_inc(const_ready, 1)

            def step(s, u, ok):
                if ok(1):
                    rstd2_of(s - 1, u - 1)
                if ok(0):
                    t, a, r = s, u % 2, u % RING
                    pool.wait_ge(srec_ready, t + 1)
                    reused(pool, mix_ready, t, 2)
                    pool.tensor_tensor(vT[:, a, :].rearrange("p (n s) -> p n s", s=SEQ),
                                       tok_sb[:, r, 2 * D:3 * D].rearrange("p (n s) -> p n s", s=SEQ),
                                       srec[:, a, :].unsqueeze(2).broadcast_to([P, HALVES * DC, SEQ]), ALU.mult
                                       ).then_inc(vT_ready, 1)
                if ok(-2) and (not isinstance(s, int) or s >= 0):
                    rstd1_of(s + 2, u + 2)
                if ok(2):
                    t, a, r = s - 2, (u - 2) % 2, (u - 2) % RING
                    pool.wait_ge(chosen_ready, t + 1)
                    if not isinstance(s, int) or t >= 1:
                        pool.wait_ge(earlier_ready, t)
                    reused(pool, rank_ready, t, RING - 1)
                    pool.tensor_tensor(earlier[:, (r + 1) % RING, :], earlier[:, r, :], chosen[:, a, :], ALU.add
                                       ).then_inc(earlier_ready, 1)

            steps(pool, step, {2: lambda: pool.wait_ge(const_ready, CONSTS)})

            def gather(e):
                r = e % XRING
                if e >= XRING:
                    pool.wait_ge(h_ready, e - XRING + 1)
                pool.indirect_dma_start(xe[r], None, table,
                                        bass.IndirectOffsetOnAxis(ap=index[:, e:e + 1], axis=0)
                                        ).then_inc(gathered[r], 16)

            def scatter(e):
                n = e % SUMS if e < EXPERTS - 1 else 0
                pool.wait_ge(ye_copied, e + 1)
                if e >= SUMS:
                    pool.wait_ge(scattered[n], 16 * (e // SUMS if e < EXPERTS - 1 else SCATTERS[0] - 1))
                pool.indirect_dma_start(sums[n], bass.IndirectOffsetOnAxis(ap=index[:, e:e + 1], axis=0),
                                        ye[:, e % RING, :], None, compute_op=ALU.add
                                        ).then_inc(scattered[n], 16)

            pool.wait_ge(index_ready, 1)
            pool.wait_ge(zeros_stored, 16 * (SUMS + 1))
            for r in range(RING):
                pool.wait_ge(row_stored[r], 16 * (TILES // RING))
                pool.wait_ge(x1_stored[r % 2], 16 * (TILES // 2))
            for e in range(LEAD):
                gather(e)
            for e in range(EXPERTS):
                if e + LEAD < EXPERTS:
                    gather(e + LEAD)
                scatter(e)
            for n in range(SUMS):
                pool.wait_ge(scattered[n], 16 * SCATTERS[n])

        @block.vector
        def _(dve):
            dve.memset(zeros, 0.0).then_inc(zeros_set, 1)

            def step(s, u, ok):
                n1, sm, n2, ro, sl = ok(-2), ok(0), ok(1), ok(2), ok(3)
                t0, a0, r0 = s + 2, (u + 2) % 2, (u + 2) % RING
                t1, a1, r1 = s, u % 2, u % RING
                t, a, r = s - 1, (u - 1) % 2, (u - 1) % RING
                t2, a2, r2 = s - 2, (u - 2) % 2, (u - 2) % RING
                t3, a3 = s - 3, (u - 3) % 2
                if sm:
                    dve.wait_ge(scores_ready, DC * (t1 + 1))
                    reused(dve, probs_ready, t1, 2, HALVES * DC)
                    dve.reduce_max(sbias[:, a1, :], scores_ps(a1).rearrange("p b (c d) -> p (b c) d", c=DC), axis=AX.X,
                                   negate=True).then_inc(sbias_ready, 1)
                if sl:
                    dve.wait_ge(rank_ready, t3 + 1)
                    dve.tensor_tensor(placed[:, a3, :], rank_ps(a3), chosen[:, a3, :], ALU.mult).then_inc(placed_ready, 1)
                if n1:
                    dve.wait_ge(tok_loaded[r0], 16 * (t0 // RING + 1) if isinstance(s, int)
                                else (t0 - r0) * (16 // RING) + 16)
                    reused(dve, xn_ready, t0, 2)
                    dve.bn_stats(stats1[:, a0, :], tok_sb[:, r0, 0:D]).then_inc(stats1_ready, 1)
                if n2:
                    dve.wait_ge(mix_ready, t + 1)
                    dma_reused(dve, x1_stored, t, a, 2)
                    dve.tensor_tensor(x1[:, a, :], mix_ps, tok_sb[:, r, 0:D], ALU.add).then_inc(x1_ready, 1)
                if sl:
                    wait_apart(dve, placed_ready, t3 + 1)
                    dve.max(dest[:, a3, :], placed[:, a3, :]).then_inc(dest_ready, 1)
                if n1:
                    wait_apart(dve, stats1_ready, t0 + 1)
                    dve.bn_aggr(mv1[:, a0, :], stats1[:, a0, :]).then_inc(mv1_ready, 1)
                if n2:
                    dve.wait_ge(x1_ready, t + 1)
                    reused(dve, row_ready, t, 2)
                    dve.bn_stats(stats2[:, a, :], x1[:, a, :]).then_inc(stats2_ready, 1)
                if sl:
                    dve.wait_ge(dest_ready, t3 + 1)
                    dve.tensor_scalar(dest_parts[:, a3, 0, :], dest[:, a3, :], KEY - 1, None, ALU.bitwise_and
                                      ).then_inc(dest_split, 1)
                    dve.tensor_scalar(dest_parts[:, a3, 1, :], dest[:, a3, :], KEY_BITS, None,
                                      ALU.logical_shift_right).then_inc(dest_split, 1)
                if n2:
                    wait_apart(dve, stats2_ready, t + 1)
                    dve.bn_aggr(mv2[:, a, :], stats2[:, a, :]).then_inc(mv2_ready, 1)
                if ro:
                    dve.wait_ge(logits_ready, t2 + 1)
                    dve.reduce_max(lbias[:, a2:a2 + 1], logits_ps(a2), axis=AX.X, negate=True).then_inc(lbias_ready, 1)
                if sl:
                    dve.wait_ge(dest_split, 2 * t3 + 2)
                    dve.tensor_copy(dest_half[:, a3, :, :], dest_parts[:, a3, :, :]).then_inc(dest_half_ready, 1)
                if sm:
                    dve.wait_ge(probs_ready, HALVES * DC * (t1 + 1))
                    reused(dve, vT_ready, t1, 2)
                    dve.reciprocal(srec[:, a1, :], ssum[:, a1, :]).then_inc(srec_ready, 1)
                if sl:
                    dve.wait_ge(dest_half_ready, t3 + 1)
                    reused(dve, index_summed, t3, 2)
                    dve.tensor_tensor(slot_hot[:, a3, :, :], slot_no[:, :, :],
                                      dest_half[:, a3, 0, :].unsqueeze(1).broadcast_to([P, CAP, TOPK]), ALU.is_equal
                                      ).then_inc(slot_hot_ready, 1)
                if ro:
                    dve.wait_ge(lexp_ready, t2 + 1)
                    dve.reciprocal(lrec[:, a2:a2 + 1], lsum[:, a2:a2 + 1]).then_inc(lrec_ready, 1)
                    dve.wait_ge(lrec_ready, t2 + 1)
                    dve.tensor_scalar(p_all[:, a2, :], lexp[:, a2, :], lrec[:, a2:a2 + 1], None, ALU.mult
                                      ).then_inc(p_ready, 1)
                if sl:
                    if not isinstance(s, int) or t3 >= 1:
                        dve.wait_ge(expert_tok_ready, t3)
                    dve.tensor_tensor(expert_hot[:, :, :], expert_no[:, :, :],
                                      dest_half[:, a3, 1, :].unsqueeze(1).broadcast_to([P, EXPERTS, TOPK]), ALU.is_equal
                                      ).then_inc(expert_hot_ready, 1)
                if ro:
                    wait_apart(dve, p_ready, t2 + 1)
                    dve.max(p_top[:, a2, :], p_all[:, a2, :]).then_inc(top_ready, 1)
                if ro:
                    wait_apart(dve, top_ready, t2 + 1)
                    dve.match_replace(p_marked[:, a2, :], p_top[:, a2, :], p_all[:, a2, :], -1.0
                                      ).then_inc(marked_ready, 1)
                    dve.reduce_sum(p_topsum[:, a2:a2 + 1], p_top[:, a2, :], axis=AX.X).then_inc(topsum_ready, 1)
                if ro:
                    dve.wait_ge(marked_ready, t2 + 1)
                    dve.tensor_scalar(chosen[:, a2, :], p_marked[:, a2, :], 0.0, None, ALU.is_lt
                                      ).then_inc(chosen_ready, 1)
                    dve.wait_ge(topsum_ready, t2 + 1)
                    dve.reciprocal(p_toprec[:, a2:a2 + 1], p_topsum[:, a2:a2 + 1]).then_inc(toprec_ready, 1)
                    dve.wait_ge(chosen_ready, t2 + 1)
                    dve.wait_ge(toprec_ready, t2 + 1)
                    dve.scalar_tensor_tensor(row[:, r2, D:ROW], p_all[:, a2, :], p_toprec[:, a2:a2 + 1],
                                             chosen[:, a2, :], ALU.mult, ALU.mult).then_inc(shares_ready, 1)

            def constants():
                for n, to in enumerate(pattern_of):
                    dve.wait_ge(pattern_ready, n + 1)
                    dve.tensor_copy(to, patterns[n]).then_inc(const_ready, 1)

            steps(dve, step, {1: constants, 3: lambda: dve.wait_ge(const_ready, CONSTS)})

            dve.wait_ge(index_summed, TILES)
            dve.tensor_scalar(empty, index_ps, 0.0, spare[:, 0:1], ALU.is_equal, ALU.mult).then_inc(empty_ready, 1)
            dve.wait_ge(empty_ready, 1)
            dve.scalar_tensor_tensor(index[:, :], index_ps, -1.0, empty, ALU.add, ALU.add
                                     ).then_inc(index_ready, 1)

            def step_e(s, u, ok):
                if ok(2):
                    e, a = s - 2, (u - 2) % 2
                    dve.wait_ge(hT_ready, e + 1)
                    reused(dve, ye_ready, e, 2)
                    dve.tensor_copy(hT[:, a, :], hT_ps(a)).then_inc(hT_copied, 1)
                if ok(1):
                    e, a, r = s - 1, (u - 1) % 2, (u - 1) % XRING
                    dve.wait_ge(sg_ready, e + 1)
                    reused(dve, hT_ready, e, 2)
                    dve.scalar_tensor_tensor(h[:, a, :], gu_ps(a)[:, INNER:2 * INNER],
                                             xe[r][:, bass.ds(e + D, 1)], sg[:, a, :], ALU.mult, ALU.mult
                                             ).then_inc(h_ready, 1)

            run(dve, step_e)

            w = span // LAST
            for c in range(LAST):
                dve.wait_ge(last_loaded[c], 16 * SUMS)
                dve.tensor_tensor(last[0][:, c * w:(c + 1) * w], last[0][:, c * w:(c + 1) * w],
                                  last[1][:, c * w:(c + 1) * w], ALU.add).then_inc(last_added, 1)

        @block.scalar
        def _(act):
            def step(s, u, ok):
                if ok(2):
                    t, a = s - 2, (u - 2) % 2
                    act.wait_ge(xnT_ready, t + 1)
                    reused(act, logits_ready, t, 2)
                    act.activation(xnT[:, a, :], xnT_ps(a), ACT.Copy).then_inc(xnT_copied, 1)
                if ok(0):
                    t, a = s, u % 2
                    act.wait_ge(sbias_ready, t + 1)
                    reused(act, mix_ready, t, 2)
                    reused(act, srec_ready, t, 2)
                    for n in range(HALVES * DC):
                        act.activation(probs[:, a, n * D:(n + 1) * D],
                                       scores_ps(a)[:, n // DC, (n % DC) * D:(n % DC + 1) * D],
                                       ACT.Exp, bias=sbias[:, a, n:n + 1], accum_out=ssum[:, a, n:n + 1]
                                       ).then_inc(probs_ready, 1)
                if ok(2):
                    t, a = s - 2, (u - 2) % 2
                    act.wait_ge(lbias_ready, t + 1)
                    reused(act, p_ready, t, 2)
                    act.activation(lexp[:, a, :], logits_ps(a), ACT.Exp, bias=lbias[:, a:a + 1],
                                   accum_out=lsum[:, a:a + 1]).then_inc(lexp_ready, 1)
                if ok(1):
                    t, a, r = s - 1, (u - 1) % 2, (u - 1) % RING
                    act.wait_ge(shift2_ready, t + 1)
                    dma_reused(act, row_stored, t, r, RING)
                    act.activation(row[:, r, 0:D], x1[:, a, :], ACT.Identity, scale=rstd2[:, a:a + 1],
                                   bias=shift2[:, a:a + 1]).then_inc(row_ready, 1)
                if ok(3):
                    t = s - 3
                    act.wait_ge(expert_hot_ready, t + 1)
                    if not isinstance(s, int) or t >= 1:
                        act.wait_ge(index_summed, t)
                    act.activation(expert_tok[:, :, :], expert_hot[:, :, :], ACT.Copy, scale=token_no[:, bass.ds(t, 1)]
                                   ).then_inc(expert_tok_ready, 1)
                if ok(-2):
                    t, a, r = s + 2, (u + 2) % 2, (u + 2) % RING
                    act.wait_ge(shift1_ready, t + 1)
                    reused(act, scores_ready, t, 2, DC)
                    act.activation(xn[:, a, :], tok_sb[:, r, 0:D], ACT.Identity, scale=rstd1[:, a:a + 1],
                                   bias=shift1[:, a:a + 1]).then_inc(xn_ready, 1)

            steps(act, step, {3: lambda: act.wait_ge(const_ready, CONSTS)})

            def step_e(s, u, ok):
                if ok(3):
                    e, a, r = s - 3, (u - 3) % 2, (u - 3) % RING
                    act.wait_ge(ye_ready, e + 1)
                    if not isinstance(e, int) or e >= RING:
                        act.wait_ge(scattered[a], ((e - RING) // SUMS + 1) * 16 if isinstance(e, int)
                                    else (e - RING - a) * (16 // SUMS) + 16)
                    act.activation(ye[:, r, :], ye_ps(a), ACT.Copy).then_inc(ye_copied, 1)
                if ok(0):
                    e, a = s, u % 2
                    act.wait_ge(xeT_ready, e + 1)
                    reused(act, gu_ready, e, 2)
                    act.activation(xeT[:, a, :], xeT_ps(a), ACT.Copy).then_inc(xeT_copied, 1)
                if ok(1):
                    e, a = s - 1, (u - 1) % 2
                    act.wait_ge(gu_ready, e + 1)
                    reused(act, h_ready, e, 2)
                    act.activation(sg[:, a, :], gu_ps(a)[:, 0:INNER], ACT.Silu).then_inc(sg_ready, 1)

            run(act, step_e)

        @block.tensor
        def _(pe):
            def scores(t, u, c):
                a, r = u % 2, u % RING
                if c == 0:
                    pe.wait_ge(xn_ready, t + 1)
                    reused(pe, probs_ready, t, 2, HALVES * DC)
                for b in range(HALVES):
                    rows = slice(b * SEQ, (b + 1) * SEQ)
                    mm = pe.matmul(scores_ps(a)[:, b, c * D:(c + 1) * D],
                                   tok_sb[rows, r, D + c * P:D + (c + 1) * P], xn[rows, a, :], start=True, stop=True)
                mm.then_inc(scores_ready, 1)

            def mix(t, u):
                a = u % 2
                pe.wait_ge(vT_ready, t + 1)
                if not isinstance(t, int) or t >= 1:
                    pe.wait_ge(x1_ready, t)
                for c in range(DC):
                    for b in range(HALVES):
                        n = b * DC + c
                        mm = pe.matmul(mix_ps[b * SEQ:(b + 1) * SEQ, :], vT[:, a, n * SEQ:(n + 1) * SEQ],
                                       probs[:, a, n * D:(n + 1) * D], start=(c == 0), stop=(c == DC - 1))
                mm.then_inc(mix_ready, 1)

            def turn(t, u):
                a, r = u % 2, u % RING
                pe.wait_ge(row_ready, t + 1)
                reused(pe, placed_ready, t, 2)
                for c in range(DC):
                    mm = pe.transpose(xnT_ps(a)[:, c * P:(c + 1) * P], row[:, r, c * P:(c + 1) * P], ident[:, :])
                mm.then_inc(xnT_ready, 1)

            def logits(t, u):
                a = u % 2
                pe.wait_ge(xnT_copied, t + 1)
                for c in range(DC):
                    mm = pe.matmul(logits_ps(a), xnT[:, a, c * P:(c + 1) * P], wr_sb[:, c, :],
                                   start=(c == 0), stop=(c == DC - 1))
                mm.then_inc(logits_ready, 1)

            def rank(t, u):
                a, r = u % 2, u % RING
                pe.wait_ge(chosen_ready, t + 1)
                if not isinstance(t, int) or t >= 1:
                    pe.wait_ge(earlier_ready, t)
                pe.matmul(rank_ps(a), ones[:, :], expert_key[:, :], start=True, stop=False)
                pe.matmul(rank_ps(a), before[:, :], chosen[:, a, :], start=False, stop=False)
                pe.matmul(rank_ps(a), ones[:, :], earlier[:, r, :], start=False, stop=True).then_inc(rank_ready, 1)

            def index_add(t, u):
                a = u % 2
                pe.wait_ge(slot_hot_ready, t + 1)
                pe.wait_ge(expert_tok_ready, t + 1)
                first = isinstance(t, int) and t == 0
                for k in range(TOPK):
                    mm = pe.matmul(index_ps, slot_hot[:, a, :, k], expert_tok[:, :, k],
                                   start=(first and k == 0),
                                   stop=(isinstance(t, int) and t == TILES - 1 and k == TOPK - 1))
                mm.then_inc(index_summed, 1)

            def step(s, u, ok):
                if ok(2):
                    turn(s - 2, u - 2)
                if ok(1):
                    mix(s - 1, u - 1)
                if ok(3):
                    rank(s - 3, u - 3)
                if ok(2):
                    logits(s - 2, u - 2)
                if ok(-1):
                    scores(s + 1, u + 1, 0)
                    scores(s + 1, u + 1, 1)
                if ok(4):
                    index_add(s - 4, u - 4)

            def constants():
                pe.wait_ge(const_ready, CONSTS)
                pe.wait_ge(wr_loaded, 16)

            steps(pe, step, {2: constants})

            pe.wait_ge(weights_loaded, 16 * 2 * GROUPS)

            def step_e(s, u, ok):
                if ok(3):
                    e, a = s - 3, (u - 3) % 2
                    pe.wait_ge(hT_copied, e + 1)
                    reused(pe, ye_copied, e, 2)
                    pe.matmul(ye_ps(a), hT[:, a, :], wd_sb[:, bass.ds(e, 1), :], start=True, stop=True
                              ).then_inc(ye_ready, 1)
                if ok(0):
                    e, a, r = s, u % 2, u % XRING
                    pe.wait_ge(gathered[r], 16 * (e // XRING + 1) if isinstance(e, int)
                               else (e - r) * (16 // XRING) + 16)
                    reused(pe, xeT_copied, e, 2)
                    for c in range(DC):
                        mm = pe.transpose(xeT_ps(a)[:, c * P:(c + 1) * P], xe[r][:, c * P:(c + 1) * P], ident[:, :])
                    mm.then_inc(xeT_ready, 1)
                if ok(2):
                    e, a = s - 2, (u - 2) % 2
                    pe.wait_ge(h_ready, e + 1)
                    reused(pe, hT_copied, e, 2)
                    pe.transpose(hT_ps(a), h[:, a, :], ident[:, :]).then_inc(hT_ready, 1)
                if ok(1):
                    e, a = s - 1, (u - 1) % 2
                    pe.wait_ge(xeT_copied, e + 1)
                    reused(pe, h_ready, e, 2)
                    for c in range(DC):
                        mm = pe.matmul(gu_ps(a), xeT[:, a, c * P:(c + 1) * P],
                                       wgu_sb[:, bass.ds(e, 1), c * 2 * INNER:(c + 1) * 2 * INNER],
                                       start=(c == 0), stop=(c == DC - 1))
                    mm.then_inc(gu_ready, 1)

            run(pe, step_e)


CONSTS = 10
SCATTERS = (EXPERTS // SUMS + 1, EXPERTS // SUMS - 1)
KEY_BITS = KEY.bit_length() - 1
SCALE = float(D) ** -0.5


def steps(eng, step, before={}):
    first = UNROLL + 1
    last = TILES - 3

    def ok_at(s):
        return lambda lag: 0 <= s - lag < TILES

    for s in range(-2, first):
        if s in before:
            before[s]()
        step(s, s, ok_at(s))
    with eng.Fori(first, last - UNROLL + 1, UNROLL) as base:
        for u in range(UNROLL):
            step(base + u, first + u, lambda lag: True)
    for s in range(last, TILES + 4):
        step(s, s, ok_at(s))


def kernel(**inputs):
    import concourse.bacc as _bacc
    from concourse.bass_utils import run_bass_kernel_spmd as _run

    x = np.asarray(inputs["x"]).reshape(TOKENS, D)
    c = np.asarray(inputs["ctx_2048"])
    cT = c.reshape(TILES, HALVES, SEQ, DC, P).transpose(0, 4, 1, 3, 2).reshape(TOKENS, D)
    gate, up = (np.asarray(inputs[n]).reshape(EXPERTS, DC, P, INNER) for n in ("L0_ffn_gate_proj", "L0_ffn_up_proj"))
    arrays = {
        "tok": np.concatenate([x, c.reshape(TOKENS, D), cT], axis=1),
        "wgu": np.stack([gate, up], axis=3).transpose(2, 0, 1, 3, 4).reshape(P, EXPERTS, DC * 2 * INNER),
        "wd": np.asarray(inputs["L0_ffn_down_proj"]).transpose(1, 0, 2),
        "wr": np.asarray(inputs["L0_ffn_router_weight"]).reshape(DC, P, EXPERTS).transpose(1, 0, 2),
    }
    arrays = {k: np.ascontiguousarray(v) for k, v in arrays.items()}
    nc = _bacc.Bacc("TRN2", target_bir_lowering=False, num_devices=1)
    args = [nc.dram_tensor(f"in_{k}", v.shape, F32, kind="ExternalInput").ap() for k, v in arrays.items()]
    out = nc.dram_tensor("out_x", (BATCH, SEQ, D), F32, kind="ExternalOutput").ap()
    build(nc, *args, out)
    r = _run(nc, [{f"in_{k}": v for k, v in arrays.items()}], core_ids=[0])
    return r.results[0]["out_x"]
```
